# Optimizing a Trainium2 kernel written in Bass

```python
import numpy as np
import jax
import jax.numpy as jnp

def _softmax(x, axis=-1):
    return jax.nn.softmax(x, axis=axis)
def _gelu(x):
    return jax.nn.gelu(x, approximate=True)
def _silu(x):
    return jax.nn.silu(x)
def _sigmoid(x):
    return jax.nn.sigmoid(x)
def _layernorm(x, axis=-1, eps=1e-5):
    m = jnp.mean(x, axis=axis, keepdims=True)
    v = jnp.var(x, axis=axis, keepdims=True)
    return (x - m) / jnp.sqrt(v + eps)
def _scatter_add(tgt, idx, src, axis=0):
    return tgt.at[idx].add(src)
def _segment_sum(src, seg, n):
    return jax.ops.segment_sum(src, seg, n)

kernel_name = 'mk_conv_seq_d2_conv_nhwc128_bca9bd'

def setup_inputs(seed: int = 0):
    np.random.seed(seed)
    _w = jnp.asarray
    def _rec_inputs():
        import jax
        import jax.numpy as jnp
        _gk = jax.random.key(seed)
        x = -0.0003482 + 1 * jax.random.normal(jax.random.fold_in(_gk, 1), (1, 384, 384, 128), jnp.float32)
        return x
    x = _rec_inputs()
    def _L0_conv_setup():
        import jax, jax.numpy as jnp
        import numpy as np
        EPS = 1e-05

        def _layernorm(x, g, b):
            mu = jnp.mean(x, axis=-1, keepdims=True)
            var = jnp.var(x, axis=-1, keepdims=True)
            return (x - mu) * jax.lax.rsqrt(var + EPS) * g + b

        def _linear(x, W, b):
            return jnp.einsum('...i,oi->...o', x, W) + b
        key = jax.random.key(seed)
        ks = jax.random.split(key, 16)
        B, L, D = (1, 384, 128)
        s = 1.0 / np.sqrt(D)
        inp = {'z': jax.random.normal(ks[0], (B, L, L, D), dtype=jnp.float32), 'norm_g': jnp.ones((D,), jnp.float32), 'norm_b': jnp.zeros((D,), jnp.float32), 'Wa': jax.random.uniform(ks[1], (D, D), jnp.float32, -s, s), 'ba': jax.random.uniform(ks[2], (D,), jnp.float32, -s, s), 'Wb': jax.random.uniform(ks[3], (D, D), jnp.float32, -s, s), 'bb': jax.random.uniform(ks[4], (D,), jnp.float32, -s, s), 'Wga': jax.random.uniform(ks[5], (D, D), jnp.float32, -s, s), 'bga': jax.random.uniform(ks[6], (D,), jnp.float32, -s, s), 'Wgb': jax.random.uniform(ks[7], (D, D), jnp.float32, -s, s), 'bgb': jax.random.uniform(ks[8], (D,), jnp.float32, -s, s), 'Wo': jax.random.uniform(ks[9], (D, D), jnp.float32, -s, s), 'bo': jax.random.uniform(ks[10], (D,), jnp.float32, -s, s), 'Wgo': jax.random.uniform(ks[11], (D, D), jnp.float32, -s, s), 'bgo': jax.random.uniform(ks[12], (D,), jnp.float32, -s, s), 'normo_g': jnp.ones((D,), jnp.float32), 'normo_b': jnp.zeros((D,), jnp.float32)}
        return inp
    _L0_conv_all = _L0_conv_setup()
    _L0_conv_in = {k: v for k, v in _L0_conv_all.items() if k in ('norm_g', 'norm_b', 'Wa', 'ba', 'Wb', 'bb', 'Wga', 'bga', 'Wgb', 'bgb', 'Wo', 'bo', 'Wgo', 'bgo', 'normo_g', 'normo_b', )}
    del _L0_conv_all

    def _L1_conv_setup():
        import jax, jax.numpy as jnp
        import numpy as np
        LN_EPS = 1e-05

        def _layer_norm(x, scale, bias):
            mu = jnp.mean(x, axis=-1, keepdims=True)
            var = jnp.mean(jnp.square(x - mu), axis=-1, keepdims=True)
            return (x - mu) * jax.lax.rsqrt(var + LN_EPS) * scale + bias
        key = jax.random.key(seed)
        ks = jax.random.split(key, 8)
        B, N, C, H = (1, 384, 128, 128)
        s_in = 1.0 / np.sqrt(C)
        s_h = 1.0 / np.sqrt(H)
        return {'pair': jax.random.normal(ks[0], (B, N, N, C), jnp.float32), 'W_left': jax.random.normal(ks[1], (C, H), jnp.float32) * s_in, 'b_left': jnp.zeros((H,), jnp.float32), 'W_right': jax.random.normal(ks[2], (C, H), jnp.float32) * s_in, 'b_right': jnp.zeros((H,), jnp.float32), 'W_gate': jax.random.normal(ks[3], (C, H), jnp.float32) * s_in, 'b_gate': jnp.zeros((H,), jnp.float32), 'W_eq': jax.random.normal(ks[4], (C, H), jnp.float32) * s_in, 'b_eq': jnp.zeros((H,), jnp.float32), 'W_out': jax.random.normal(ks[5], (H, C), jnp.float32) * s_h, 'b_out': jnp.zeros((C,), jnp.float32), 'ln_scale': jnp.ones((C,), jnp.float32), 'ln_bias': jnp.zeros((C,), jnp.float32)}
    _L1_conv_all = _L1_conv_setup()
    _L1_conv_in = {k: v for k, v in _L1_conv_all.items() if k in ('W_left', 'b_left', 'W_right', 'b_right', 'W_gate', 'b_gate', 'W_eq', 'b_eq', 'W_out', 'b_out', 'ln_scale', 'ln_bias', )}
    del _L1_conv_all

    return {
        "x": x,
        "L0_conv_norm_g": _L0_conv_in["norm_g"],
        "L0_conv_norm_b": _L0_conv_in["norm_b"],
        "L0_conv_Wa": _L0_conv_in["Wa"],
        "L0_conv_ba": _L0_conv_in["ba"],
        "L0_conv_Wb": _L0_conv_in["Wb"],
        "L0_conv_bb": _L0_conv_in["bb"],
        "L0_conv_Wga": _L0_conv_in["Wga"],
        "L0_conv_bga": _L0_conv_in["bga"],
        "L0_conv_Wgb": _L0_conv_in["Wgb"],
        "L0_conv_bgb": _L0_conv_in["bgb"],
        "L0_conv_Wo": _L0_conv_in["Wo"],
        "L0_conv_bo": _L0_conv_in["bo"],
        "L0_conv_Wgo": _L0_conv_in["Wgo"],
        "L0_conv_bgo": _L0_conv_in["bgo"],
        "L0_conv_normo_g": _L0_conv_in["normo_g"],
        "L0_conv_normo_b": _L0_conv_in["normo_b"],
        "L1_conv_W_left": _L1_conv_in["W_left"],
        "L1_conv_b_left": _L1_conv_in["b_left"],
        "L1_conv_W_right": _L1_conv_in["W_right"],
        "L1_conv_b_right": _L1_conv_in["b_right"],
        "L1_conv_W_gate": _L1_conv_in["W_gate"],
        "L1_conv_b_gate": _L1_conv_in["b_gate"],
        "L1_conv_W_eq": _L1_conv_in["W_eq"],
        "L1_conv_b_eq": _L1_conv_in["b_eq"],
        "L1_conv_W_out": _L1_conv_in["W_out"],
        "L1_conv_b_out": _L1_conv_in["b_out"],
        "L1_conv_ln_scale": _L1_conv_in["ln_scale"],
        "L1_conv_ln_bias": _L1_conv_in["ln_bias"],
    }

def reference(x, L0_conv_norm_g, L0_conv_norm_b, L0_conv_Wa, L0_conv_ba, L0_conv_Wb, L0_conv_bb, L0_conv_Wga, L0_conv_bga, L0_conv_Wgb, L0_conv_bgb, L0_conv_Wo, L0_conv_bo, L0_conv_Wgo, L0_conv_bgo, L0_conv_normo_g, L0_conv_normo_b, L1_conv_W_left, L1_conv_b_left, L1_conv_W_right, L1_conv_b_right, L1_conv_W_gate, L1_conv_b_gate, L1_conv_W_eq, L1_conv_b_eq, L1_conv_W_out, L1_conv_b_out, L1_conv_ln_scale, L1_conv_ln_bias):
    import jax
    import jax.numpy as jnp
    def _L0_conv_ref(z, norm_g, norm_b, Wa, ba, Wb, bb, Wga, bga, Wgb, bgb, Wo, bo, Wgo, bgo, normo_g, normo_b):
        import jax, jax.numpy as jnp
        import numpy as np
        EPS = 1e-05

        def _layernorm(x, g, b):
            mu = jnp.mean(x, axis=-1, keepdims=True)
            var = jnp.var(x, axis=-1, keepdims=True)
            return (x - mu) * jax.lax.rsqrt(var + EPS) * g + b

        def _linear(x, W, b):
            return jnp.einsum('...i,oi->...o', x, W) + b
        z_n = _layernorm(z, norm_g, norm_b)
        a = _linear(z_n, Wa, ba) * jax.nn.sigmoid(_linear(z_n, Wga, bga))
        b = _linear(z_n, Wb, bb) * jax.nn.sigmoid(_linear(z_n, Wgb, bgb))
        x = jnp.einsum('bijd,bjkd->bikd', a, b)
        x = _layernorm(x, normo_g, normo_b)
        return z + _linear(x, Wo, bo) * jax.nn.sigmoid(_linear(z_n, Wgo, bgo))

    def _L1_conv_ref(pair, W_left, b_left, W_right, b_right, W_gate, b_gate, W_eq, b_eq, W_out, b_out, ln_scale, ln_bias):
        import jax, jax.numpy as jnp
        import numpy as np
        LN_EPS = 1e-05

        def _layer_norm(x, scale, bias):
            mu = jnp.mean(x, axis=-1, keepdims=True)
            var = jnp.mean(jnp.square(x - mu), axis=-1, keepdims=True)
            return (x - mu) * jax.lax.rsqrt(var + LN_EPS) * scale + bias
        left = pair @ W_left + b_left
        right = pair @ W_right + b_right
        gate = jax.nn.sigmoid(pair @ W_gate + b_gate)
        left = left + (pair @ W_eq + b_eq)
        right_sum = jnp.sum(right, axis=2, keepdims=True)
        out = left * right_sum
        out = out * gate
        out = out @ W_out + b_out
        return _layer_norm(out + pair, ln_scale, ln_bias)

    def _gn(v, G=32, eps=1e-5):
        B_, H_, W_, C_ = v.shape
        g = v.reshape(B_, H_, W_, G, C_ // G)
        m = jnp.mean(g, axis=(1, 2, 4), keepdims=True)
        s = jnp.var(g, axis=(1, 2, 4), keepdims=True)
        return ((g - m) / jnp.sqrt(s + eps)).reshape(v.shape)

    def _ln_c(v, eps=1e-6):
        m = jnp.mean(v, axis=-1, keepdims=True)
        s = jnp.var(v, axis=-1, keepdims=True)
        return (v - m) / jnp.sqrt(s + eps)

    def _ln_t(v, eps=1e-5):
        m = jnp.mean(v, axis=-1, keepdims=True)
        s = jnp.var(v, axis=-1, keepdims=True)
        return (v - m) / jnp.sqrt(s + eps)

    def _to_tokens(v):
        B_, H_, W_, C_ = v.shape
        return v.reshape(B_, H_ * W_, C_)
    def _from_tokens(t, like):
        return t.reshape(like.shape)

    x = _L0_conv_ref(x, L0_conv_norm_g, L0_conv_norm_b, L0_conv_Wa, L0_conv_ba, L0_conv_Wb, L0_conv_bb, L0_conv_Wga, L0_conv_bga, L0_conv_Wgb, L0_conv_bgb, L0_conv_Wo, L0_conv_bo, L0_conv_Wgo, L0_conv_bgo, L0_conv_normo_g, L0_conv_normo_b)
    x = _L1_conv_ref(x, L1_conv_W_left, L1_conv_b_left, L1_conv_W_right, L1_conv_b_right, L1_conv_W_gate, L1_conv_b_gate, L1_conv_W_eq, L1_conv_b_eq, L1_conv_W_out, L1_conv_b_out, L1_conv_ln_scale, L1_conv_ln_bias)
    return x


_drawn_inputs = setup_inputs


def setup_inputs(seed=0):
    import zlib

    import numpy as np

    out = dict(_drawn_inputs(seed))
    spreads = {'L0_conv_norm_g': (1.0, 0.2),
     'L0_conv_norm_b': (0.0, 0.1),
     'L0_conv_normo_g': (1.0, 0.2),
     'L0_conv_normo_b': (0.0, 0.1),
     'L1_conv_b_left': (0.0, 0.1),
     'L1_conv_b_right': (0.0, 0.1),
     'L1_conv_b_gate': (0.0, 0.1),
     'L1_conv_b_eq': (0.0, 0.1),
     'L1_conv_b_out': (0.0, 2.0),
     'L1_conv_ln_scale': (1.0, 0.2),
     'L1_conv_ln_bias': (0.0, 0.1)}
    factors = {'L0_conv_bga': 3.422, 'L0_conv_bgb': 3.918, 'L0_conv_bgo': 4.098}
    for name, (base, spread) in spreads.items():
        noise = np.random.default_rng([zlib.crc32(name.encode()), seed]).standard_normal(out[name].shape)
        drawn = base * np.exp(spread * noise) if base else spread * noise
        out[name] = jnp.asarray(drawn.astype(out[name].dtype))
    for name, factor in factors.items():
        out[name] = (out[name] * factor).astype(out[name].dtype)
    return out
```

```python
from contextlib import ExitStack

import concourse.bass as bass
from concourse import mybir

F32 = mybir.dt.float32
F32R = mybir.dt.float32r
ALU = mybir.AluOpType
ACT = mybir.ActivationFunctionType

P = 128
D = 128
L = 384
LB = L // P
TOKENS = L * L
EPS = 1e-5

GT = 4
GROUP = GT * P
GROUPS = TOKENS // GROUP
LOAD_G = 2
LOAD_RING = 6
BATCH_G = 4
BODY_G = 12
BATCH_RING = BODY_G // BATCH_G
STATS_AHEAD = 8
NORM_POOL = 3

CR = 4
CT = CR * LB
CHUNKS = L // CR
CRING = 3
BODY_R = CR * CRING
X_AHEAD = 6
NORM_BEHIND = 7


def wait(engine, semaphore, value):
    if isinstance(value, int) and value <= 0:
        return
    engine.wait_ge(semaphore, value)


MOMENT_STEPS = 5


def moments(dve, stats, work, steps, base):
    double_mean, total, square = work
    dve.tensor_tensor(double_mean, stats[..., 1], stats[..., 4], ALU.subtract).then_inc(steps, 1)
    dve.tensor_tensor(total, stats[..., 2], stats[..., 5], ALU.add).then_inc(steps, 1)
    dve.wait_ge(steps, base + 1)
    dve.scalar_tensor_tensor(square, double_mean, D / 4.0, double_mean, ALU.mult, ALU.mult)\
        .then_inc(steps, 1)
    dve.wait_ge(steps, base + 3)
    dve.tensor_tensor(total, total, square, ALU.add).then_inc(steps, 1)
    dve.tensor_tensor(double_mean, stats[..., 1], stats[..., 4], ALU.add).then_inc(steps, 1)


def bass_pair_layers(nc, x, w, vec, out):
    a_dram = nc.dram_tensor("a_scratch", (D, TOKENS), F32, kind="Internal").ap()
    b_dram = nc.dram_tensor("b_scratch", (D, TOKENS), F32, kind="Internal").ap()
    x_dram = nc.dram_tensor("x_scratch", (D, TOKENS), F32, kind="Internal").ap()
    z_flat = x.rearrange("b i j c -> (b i j) c")
    out_flat = out.rearrange("b i j c -> (b i j) c")

    with ExitStack() as ctx:
        def sb(name, shape, dt=F32):
            return ctx.enter_context(nc.sbuf_tensor(name, shape, dt))

        const = {
            "identity": sb("identity", [P, P]),
            "rstd_z": sb("rstd_z", [P, TOKENS // P]),
        }
        for n in ("Wa", "Wga", "Wb", "Wgb"):
            const[n + "_high"] = sb(n + "_high", [D, D], F32R)
            const[n + "_low"] = sb(n + "_low", [D, D], F32R)
        for n in ("Wgo", "Wo", "Wle", "Wg", "Wr", "Wout"):
            const[n] = sb(n + "_c", [D, D])
        for n in ("ba", "bga", "bb", "bgb", "ble", "bg", "br"):
            const[n] = sb(n + "_col", [D, 1])
        for n in ("bgo", "bo"):
            const[n] = sb(n + "_row", [P, D])
        for n in ("bout", "ln_scale", "ln_bias"):
            const[n] = sb(n + "_row", [P, LB * D])

        prepare(nc, w, vec, const)
        project(nc, z_flat, a_dram, b_dram, const)
        triangle(nc, a_dram, b_dram, x_dram, const)
        finish(nc, z_flat, x_dram, out_flat, const)


def prepare(nc, w, vec, const):
    with ExitStack() as ctx:
        def sb(name, shape, dt=F32):
            return ctx.enter_context(nc.sbuf_tensor(name, shape, dt))

        def sem(name):
            return ctx.enter_context(nc.semaphore(name))

        gated = ("Wa", "Wga", "Wb", "Wgb")
        raw = {n: sb("raw_" + n, [D, D]) for n in (*gated, "Wgo", "Wo", "Wl", "We")}
        scaled = {n: sb("scaled_" + n, [D, D]) for n in (*gated, "Wgo", "Wo")}
        col = {n: sb("col_" + n, [D, 1]) for n in
               ("norm_g", "norm_b", "normo_g", "normo_b", "ba", "bga", "bb", "bgb", "bl", "be", "br")}
        row = {n: sb("row_" + n, [P, D]) for n in ("bgo", "bo")}
        spread = {n: sb("spread_" + n, [D, P]) for n in ("norm_b", "normo_b")}
        ones = sb("ones", [D, P])
        inv_d = sb("inv_d", [D, P])
        psum_col = ctx.enter_context(nc.psum_tensor("prep_col", [D, 4], F32))
        psum_row = [ctx.enter_context(nc.psum_tensor(f"prep_row{k}", [P, D], F32)) for k in range(2)]
        psum_mean = [ctx.enter_context(nc.psum_tensor(f"prep_mean{k}", [P, D], F32)) for k in range(2)]

        loaded = sem("prep_loaded")
        filled = sem("prep_filled")
        chain = sem("prep_chain")
        multiplied = sem("prep_multiplied")
        block = ctx.enter_context(nc.Block())

        def column(v):
            return v.rearrange("(c o) -> c o", o=1)

        def spread_row(v):
            return v.rearrange("(o c) -> o c", o=1).partition_broadcast(P)

        loads = [(raw[n][:], w[n]) for n in raw]
        loads += [(const[n][:], w[n]) for n in ("Wg", "Wr", "Wout")]
        loads += [(col[n][:], column(vec[n])) for n in col]
        loads += [(const["bg"][:], column(vec["bg"]))]
        loads += [(row[n][:], spread_row(vec[n])) for n in row]
        loads += [(const[n][:, k * D:(k + 1) * D], spread_row(vec[n]))
                  for n in ("bout", "ln_scale", "ln_bias") for k in range(LB)]

        @block.sync
        def _(sp):
            for to, of in loads:
                sp.dma_start(to, of).then_inc(loaded, 16)

        @block.gpsimd
        def _(pool):
            pool.memset(const["identity"][:], 0.0).then_inc(filled, 1)
            pool.wait_ge(filled, 1)
            pool.affine_select(out=const["identity"][:], in_=const["identity"][:],
                               compare_op=ALU.not_equal, fill=1.0, base=0,
                               pattern=[[-1, P]], channel_multiplier=1).then_inc(filled, 1)

        @block.vector
        def _(dve):
            count = [0]

            def step(ins):
                ins.then_inc(chain, 1)
                count[0] += 1

            def settle():
                dve.wait_ge(chain, count[0])

            step(dve.memset(ones[:], 1.0))
            step(dve.memset(inv_d[:], 1.0 / D))
            settle()
            dve.wait_ge(loaded, 16 * len(loads))
            for n, v in (("norm_b", "norm_b"), ("normo_b", "normo_b")):
                step(dve.tensor_scalar(spread[n][:], ones[:], col[v][:, 0:1], None, ALU.mult))
            for n in (*gated, "Wgo"):
                step(dve.tensor_scalar(scaled[n][:], raw[n][:], col["norm_g"][:, 0:1], None, ALU.mult))
            step(dve.tensor_scalar(scaled["Wo"][:], raw["Wo"][:], col["normo_g"][:, 0:1], None, ALU.mult))
            step(dve.tensor_tensor(const["Wle"][:], raw["Wl"][:], raw["We"][:], ALU.add))
            step(dve.tensor_tensor(const["ble"][:], col["bl"][:], col["be"][:], ALU.add))
            step(dve.tensor_scalar(const["br"][:], col["br"][:], float(L), None, ALU.mult))
            settle()
            assert count[0] == SCALED
            for n in gated:
                step(dve.tensor_copy(const[n + "_high"][:], scaled[n][:]))
            settle()
            for n in gated:
                step(dve.tensor_tensor(const[n + "_low"][:], scaled[n][:],
                                       const[n + "_high"][:].bitcast(F32), ALU.subtract))
            dve.wait_ge(multiplied, 8)
            for k, n in enumerate(("ba", "bga", "bb", "bgb")):
                step(dve.tensor_tensor(const[n][:], psum_col[:, k:k + 1], col[n][:], ALU.add))
            for k, n in enumerate(("bgo", "bo")):
                step(dve.tensor_tensor(const[n][:], psum_row[k][:], row[n][:], ALU.add))
            for k, n in enumerate(("Wgo", "Wo")):
                step(dve.tensor_tensor(const[n][:], scaled[n][:], psum_mean[k][:], ALU.subtract))
            settle()

        @block.tensor
        def _(pe):
            pe.wait_ge(loaded, 16 * len(loads))
            pe.wait_ge(chain, SCALED)
            for k, n in enumerate(gated):
                pe.matmul(psum_col[:, k:k + 1], raw[n][:], col["norm_b"][:], start=True, stop=True)\
                    .then_inc(multiplied, 1)
            for k, (n, v) in enumerate((("Wgo", "norm_b"), ("Wo", "normo_b"))):
                pe.matmul(psum_row[k][:], spread[v][:], raw[n][:], start=True, stop=True)\
                    .then_inc(multiplied, 1)
                pe.matmul(psum_mean[k][:], inv_d[:], scaled[n][:], start=True, stop=True)\
                    .then_inc(multiplied, 1)


SCALED = 2 + 2 + 5 + 1 + 3


def project(nc, z_flat, a_dram, b_dram, const):
    z_view = z_flat.rearrange("(n t p) c -> n p t c", p=P, t=LOAD_G * GT)
    batch = BATCH_G * GROUP
    tiles = BATCH_G * GT
    stats_ops = tiles + MOMENT_STEPS + 2
    factor_ops = 3

    with ExitStack() as ctx:
        def sb(name, shape, dt=F32):
            return ctx.enter_context(nc.sbuf_tensor(name, shape, dt))

        def ps(name):
            return ctx.enter_context(nc.psum_tensor(name, [P, GROUP], F32))

        def sem(name):
            return ctx.enter_context(nc.semaphore(name))

        z = [sb(f"z{k}", [P, LOAD_G * GT, D]) for k in range(LOAD_RING)]
        stats = [sb(f"stats{k}", [P, tiles, 6]) for k in range(BATCH_RING)]
        work = [[sb(f"stats_work{k}_{n}", [P, tiles]) for n in range(3)] for k in range(BATCH_RING)]
        power = sb("power", [P, tiles])
        rstd = [sb(f"rstd{k}", [P, tiles]) for k in range(BATCH_RING)]
        shift = [sb(f"shift{k}", [P, tiles]) for k in range(BATCH_RING)]
        zn = [sb(f"zn{k}", [P, GROUP]) for k in range(4)]
        zt_high = [sb(f"zt_high{k}", [D, GROUP], F32R) for k in range(2)]
        zt_low = [sb(f"zt_low{k}", [D, GROUP], F32R) for k in range(2)]
        gate = [sb(f"gate{k}", [D, GROUP]) for k in range(2)]
        gated_out = [[sb(f"gated{h}_{k}", [D, batch]) for k in range(BATCH_RING)] for h in range(2)]
        ps_zt = [ps(f"ps_zt{k}") for k in range(2)]
        ps_gate = [ps(f"ps_gate{k}") for k in range(2)]
        ps_lin = [ps(f"ps_lin{k}") for k in range(4)]

        z_loaded = [sem(f"z_loaded{k}") for k in range(LOAD_RING)]
        stats_steps = sem("stats_steps")
        factor_steps = sem("factor_steps")
        power_filled = sem("power_filled")
        normed = sem("normed")
        normed_pool = sem("normed_pool")
        scaled_pool = sem("scaled_pool")
        transposed = sem("transposed")
        high_done = sem("high_done")
        low_done = sem("low_done")
        multiplied = sem("multiplied")
        sigmoid_done = sem("sigmoid_done")
        gated = sem("gated")
        stored = [[sem(f"stored{h}_{k}") for k in range(BATCH_RING)] for h in range(2)]
        block = ctx.enter_context(nc.Block())

        weights = [("Wga", "Wa"), ("Wgb", "Wb")]
        biases = [("bga", "ba"), ("bgb", "bb")]
        loads_per_body = BODY_G // LOAD_G
        batches_per_body = BODY_G // BATCH_G
        bodies = GROUPS // BODY_G

        def run(engine, body):
            body(0, True, False)
            with engine.Fori(1, bodies - 1) as it:
                body(it, False, False)
            body(bodies - 1, False, True)

        def exists(g, last):
            return not last or g < BODY_G

        @block.sync
        def _(sp):
            def load(it, k):
                wait(sp, normed, it * BODY_G + LOAD_G * (k - LOAD_RING + 1))
                wait(sp, normed_pool, it * BODY_G + LOAD_G * (k - LOAD_RING + 1))
                sp.dma_start(z[k % LOAD_RING][:], z_view[it * loads_per_body + k])\
                    .then_inc(z_loaded[k % LOAD_RING], 16)

            def body(it, first, last):
                for j in range(batches_per_body):
                    for k in range(2 * j, 2 * j + 2):
                        if not last:
                            load(it, k + LOAD_RING)
                    for h, to in enumerate((a_dram, b_dram)):
                        sp.wait_ge(gated, it * 2 * BODY_G + 2 * BATCH_G * (j + 1) - 1 + h)
                        sp.dma_start(to[:, bass.ds((it * batches_per_body + j) * batch, batch)],
                                     gated_out[h][j][:]).then_inc(stored[h][j], 16)

            for k in range(LOAD_RING):
                load(0, k)
            run(sp, body)
            for h in range(2):
                for k in range(BATCH_RING):
                    sp.wait_ge(stored[h][k], 16 * bodies)

        @block.vector
        def _(dve):
            def measure(it, g):
                k = g // LOAD_G
                if g % LOAD_G == 0:
                    dve.wait_ge(z_loaded[k % LOAD_RING], (it + k // LOAD_RING + 1) * 16)
                for t in range(GT):
                    dve.bn_stats(stats[(g // BATCH_G) % BATCH_RING][:, (g % BATCH_G) * GT + t, :],
                                 z[k % LOAD_RING][:, (g % LOAD_G) * GT + t, :]).then_inc(stats_steps, 1)

            def close(it, b):
                k = b % BATCH_RING
                base = (it * batches_per_body + b) * stats_ops + tiles
                dve.wait_ge(stats_steps, base)
                wait(dve, factor_steps, (it * batches_per_body + b - BATCH_RING + 1) * factor_ops)
                moments(dve, stats[k][:], [x[:] for x in work[k]], stats_steps, base)
                dve.wait_ge(stats_steps, base + MOMENT_STEPS)
                dve.tensor_scalar(work[k][1][:], work[k][1][:], 1.0 / D, EPS, ALU.mult, ALU.add)\
                    .then_inc(stats_steps, 1)
                dve.tensor_scalar(work[k][0][:], work[k][0][:], -0.5, None, ALU.mult)\
                    .then_inc(stats_steps, 1)

            def low(it, g):
                dve.wait_ge(high_done, it * BODY_G + g + 1)
                dve.tensor_tensor(zt_low[g % 2][:], ps_zt[g % 2][:], zt_high[g % 2][:].bitcast(F32),
                                  ALU.subtract).then_inc(low_done, 1)

            def apply_gate(it, g, h):
                u = 2 * g + h
                if g % BATCH_G == 0:
                    wait(dve, stored[h][g // BATCH_G], 16 * it)
                dve.wait_ge(sigmoid_done, it * 2 * BODY_G + u + 1)
                dve.wait_ge(multiplied, it * 4 * BODY_G + 2 * u + 2)
                at = (g % BATCH_G) * GROUP
                dve.scalar_tensor_tensor(gated_out[h][g // BATCH_G][:, at:at + GROUP],
                                         ps_lin[u % 4][:], const[biases[h][1]][:, 0:1],
                                         gate[u % 2][:], ALU.add, ALU.mult).then_inc(gated, 1)

            def body(it, first, last):
                for g in range(BODY_G):
                    if exists(g + 1, last):
                        low(it, g + 1)
                    if exists(g + STATS_AHEAD, last):
                        measure(it, g + STATS_AHEAD)
                        if (g + STATS_AHEAD) % BATCH_G == BATCH_G - 1:
                            close(it, (g + STATS_AHEAD) // BATCH_G)
                    for h in range(2):
                        apply_gate(it, g, h)

            for g in range(STATS_AHEAD):
                measure(0, g)
                if g % BATCH_G == BATCH_G - 1:
                    close(0, g // BATCH_G)
            low(0, 0)
            run(dve, body)

        @block.scalar
        def _(act):
            def normalise(it, g):
                b = g // BATCH_G
                if g % BATCH_G == 0:
                    act.wait_ge(factor_steps, (it * batches_per_body + b) * factor_ops + 2)
                wait(act, transposed, it * BODY_G + g - 3)
                tiles_here = [t for t in range(GT) if t != NORM_POOL]
                for t in tiles_here:
                    n = (g % BATCH_G) * GT + t
                    last = act.activation(zn[g % 4][:, t * D:(t + 1) * D],
                                          z[(g // LOAD_G) % LOAD_RING][:, (g % LOAD_G) * GT + t, :],
                                          ACT.Identity, bias=shift[b % BATCH_RING][:, n:n + 1],
                                          scale=rstd[b % BATCH_RING][:, n:n + 1])
                last.then_inc(normed, 1)

            def high(it, g):
                act.wait_ge(transposed, it * BODY_G + g + 1)
                wait(act, multiplied, it * 4 * BODY_G + 4 * (g - 1))
                act.activation(zt_high[g % 2][:], ps_zt[g % 2][:], ACT.Identity).then_inc(high_done, 1)

            def sigmoid(it, g, h):
                u = 2 * g + h
                act.wait_ge(multiplied, it * 4 * BODY_G + 2 * u + 1)
                wait(act, gated, it * 2 * BODY_G + u - 1)
                act.activation(gate[u % 2][:], ps_gate[u % 2][:], ACT.Sigmoid,
                               bias=const[biases[h][0]][:, 0:1]).then_inc(sigmoid_done, 1)

            def body(it, first, last):
                for g in range(BODY_G):
                    if exists(g + 1, last):
                        high(it, g + 1)
                    if exists(g + 2, last):
                        normalise(it, g + 2)
                    for h in range(2):
                        sigmoid(it, g, h)

            normalise(0, 0)
            normalise(0, 1)
            high(0, 0)
            run(act, body)

        @block.gpsimd
        def _(pool):
            def factors(it, b):
                k = b % BATCH_RING
                n = it * batches_per_body + b
                pool.wait_ge(stats_steps, (n + 1) * stats_ops)
                wait(pool, normed, it * BODY_G + BATCH_G * (b - BATCH_RING + 1))
                wait(pool, normed_pool, it * BODY_G + BATCH_G * (b - BATCH_RING + 1))
                pool.tensor_tensor(rstd[k][:], work[k][1][:], power[:], ALU.pow).then_inc(factor_steps, 1)
                pool.wait_ge(factor_steps, n * factor_ops + 1)
                pool.tensor_tensor(shift[k][:], work[k][0][:], rstd[k][:], ALU.mult).then_inc(factor_steps, 1)
                pool.tensor_copy(const["rstd_z"][:, bass.ds(n * tiles, tiles)], rstd[k][:])\
                    .then_inc(factor_steps, 1)

            def normalise(it, g):
                b = g // BATCH_G
                if g % BATCH_G == 0:
                    pool.wait_ge(factor_steps, (it * batches_per_body + b) * factor_ops + 2)
                wait(pool, transposed, it * BODY_G + g - 3)
                t = NORM_POOL
                n = (g % BATCH_G) * GT + t
                to = zn[g % 4][:, t * D:(t + 1) * D]
                pool.tensor_tensor(to, z[(g // LOAD_G) % LOAD_RING][:, (g % LOAD_G) * GT + t, :],
                                   rstd[b][:, n:n + 1].to_broadcast([P, D]), ALU.mult).then_inc(scaled_pool, 1)
                pool.wait_ge(scaled_pool, it * BODY_G + g + 1)
                pool.tensor_tensor(to, to, shift[b][:, n:n + 1].to_broadcast([P, D]), ALU.add)\
                    .then_inc(normed_pool, 1)

            def body(it, first, last):
                for g in range(BODY_G):
                    if g % BATCH_G == 0:
                        factors(it, g // BATCH_G)
                    normalise(it, g)

            pool.memset(power[:], -0.5).then_inc(power_filled, 1)
            pool.wait_ge(power_filled, 1)
            run(pool, body)

        @block.tensor
        def _(pe):
            def transpose(it, g):
                pe.wait_ge(normed, it * BODY_G + g + 1)
                pe.wait_ge(normed_pool, it * BODY_G + g + 1)
                wait(pe, low_done, it * BODY_G + g - 1)
                for t in range(GT):
                    last = pe.transpose(ps_zt[g % 2][:, t * P:(t + 1) * P], zn[g % 4][:, t * D:(t + 1) * D],
                                        const["identity"][:])
                last.then_inc(transposed, 1)

            def multiply(it, g):
                pe.wait_ge(low_done, it * BODY_G + g + 1)
                for h in range(2):
                    u = 2 * g + h
                    for name, bank, free, count in (
                            (weights[h][0], ps_gate[u % 2], sigmoid_done, u - 1),
                            (weights[h][1], ps_lin[u % 4], gated, u - 3)):
                        wait(pe, free, it * 2 * BODY_G + count)
                        w_high, w_low = const[name + "_high"], const[name + "_low"]
                        pe.matmul(bank[:], w_low[:], zt_high[g % 2][:], start=True, stop=False)
                        pe.matmul(bank[:], w_high[:], zt_low[g % 2][:], start=False, stop=False)
                        pe.matmul(bank[:], w_high[:], zt_high[g % 2][:], start=False, stop=True)\
                            .then_inc(multiplied, 1)

            def body(it, first, last):
                for g in range(BODY_G):
                    if exists(g + 1, last):
                        transpose(it, g + 1)
                    multiply(it, g)

            transpose(0, 0)
            run(pe, body)


def triangle(nc, a_dram, b_dram, x_dram, const):
    a_view = a_dram.rearrange("d (n p j) -> d p n j", p=P, n=LB)
    b_view = b_dram.rearrange("d (n p j) -> d p n j", p=P, n=LB)
    x_view = x_dram.rearrange("d (n p j) -> d p n j", p=P, n=LB)
    ring = 4

    with ExitStack() as ctx:
        def sb(name, shape, dt=F32):
            return ctx.enter_context(nc.sbuf_tensor(name, shape, dt))

        def ps(name):
            return ctx.enter_context(nc.psum_tensor(name, [P, 512], F32))

        def sem(name):
            return ctx.enter_context(nc.semaphore(name))

        a_raw = [sb(f"a_raw{k}", [P, LB, L]) for k in range(ring)]
        b_raw = [sb(f"b_raw{k}", [P, LB, L]) for k in range(ring)]
        at_high = [sb(f"at_high{k}", [P, LB, L], F32R) for k in range(2)]
        at_low = [sb(f"at_low{k}", [P, LB, L], F32R) for k in range(2)]
        b_high = [sb(f"b_high{k}", [P, LB, L], F32R) for k in range(2)]
        b_low = [sb(f"b_low{k}", [P, LB, L], F32R) for k in range(2)]
        x_out = [sb(f"x_out{k}", [P, LB, L]) for k in range(2)]
        ps_at = [ps(f"ps_at{k}") for k in range(LB)]
        ps_x = [ps(f"ps_x{k}") for k in range(LB)]

        a_loaded = [sem(f"a_loaded{k}") for k in range(ring)]
        b_loaded = [sem(f"b_loaded{k}") for k in range(ring)]
        a_transposed = sem("a_transposed")
        a_high_done = sem("a_high_done")
        a_low_done = sem("a_low_done")
        x_multiplied = sem("x_multiplied")
        x_copied = sem("x_copied")
        b_high_done = sem("b_high_done")
        b_low_done = sem("b_low_done")
        x_stored = [sem(f"x_stored{k}") for k in range(2)]
        block = ctx.enter_context(nc.Block())
        bodies = D // ring

        def run(engine, body):
            body(0, False)
            with engine.Fori(1, bodies - 1) as it:
                body(it, False)
            body(bodies - 1, True)

        def exists(d, last):
            return not last or d < ring

        @block.sync
        def _(sp):
            def load(it, d):
                wait(sp, a_transposed, (it * ring + d - ring + 1) * LB)
                sp.dma_start(a_raw[d % ring][:], a_view[it * ring + d]).then_inc(a_loaded[d % ring], 16)
                wait(sp, b_low_done, it * ring + d - ring + 1)
                sp.dma_start(b_raw[d % ring][:], b_view[it * ring + d]).then_inc(b_loaded[d % ring], 16)

            def body(it, last):
                for d in range(ring):
                    if exists(d + ring, last):
                        load(it, d + ring)
                    sp.wait_ge(x_copied, (it * ring + d + 1) * LB)
                    sp.dma_start(x_view[it * ring + d], x_out[d % 2][:]).then_inc(x_stored[d % 2], 16)

            for d in range(ring):
                load(0, d)
            run(sp, body)
            for k in range(2):
                sp.wait_ge(x_stored[k], 16 * D // 2)

        @block.vector
        def _(dve):
            def split(it, d):
                n = it * ring + d
                dve.wait_ge(b_loaded[d % ring], (it + d // ring + 1) * 16)
                wait(dve, x_multiplied, (n - 1) * LB)
                dve.tensor_copy(b_high[d % 2][:], b_raw[d % ring][:]).then_inc(b_high_done, 1)
                for j in range(LB):
                    dve.wait_ge(a_high_done, n * LB + j + 1)
                    dve.tensor_tensor(at_low[d % 2][:, j], ps_at[j][:, 0:L],
                                      at_high[d % 2][:, j].bitcast(F32), ALU.subtract)\
                        .then_inc(a_low_done, 1)
                dve.wait_ge(b_high_done, n + 1)
                dve.tensor_tensor(b_low[d % 2][:], b_raw[d % ring][:], b_high[d % 2][:].bitcast(F32),
                                  ALU.subtract).then_inc(b_low_done, 1)

            def body(it, last):
                for d in range(ring):
                    if exists(d + 1, last):
                        split(it, d + 1)

            split(0, 0)
            run(dve, body)

        @block.scalar
        def _(act):
            def high(it, d):
                n = it * ring + d
                wait(act, x_multiplied, (n - 1) * LB)
                for j in range(LB):
                    act.wait_ge(a_transposed, n * LB + j + 1)
                    act.activation(at_high[d % 2][:, j], ps_at[j][:, 0:L], ACT.Identity)\
                        .then_inc(a_high_done, 1)

            def copy(it, d):
                n = it * ring + d
                wait(act, x_stored[d % 2], (it * (ring // 2) + d // 2) * 16)
                for i in range(LB):
                    act.wait_ge(x_multiplied, n * LB + i + 1)
                    act.activation(x_out[d % 2][:, i], ps_x[i][:, 0:L], ACT.Identity)\
                        .then_inc(x_copied, 1)

            def body(it, last):
                for d in range(ring):
                    if exists(d + 1, last):
                        high(it, d + 1)
                    copy(it, d)

            high(0, 0)
            run(act, body)

        @block.tensor
        def _(pe):
            def transpose(it, d):
                n = it * ring + d
                pe.wait_ge(a_loaded[d % ring], (it + d // ring + 1) * 16)
                for j in range(LB):
                    wait(pe, a_low_done, (n - 1) * LB + j + 1)
                    for i in range(LB):
                        last = pe.transpose(ps_at[j][:, i * P:(i + 1) * P],
                                            a_raw[d % ring][:, i, j * P:(j + 1) * P], const["identity"][:])
                    last.then_inc(a_transposed, 1)

            def multiply(it, d):
                n = it * ring + d
                pe.wait_ge(a_low_done, (n + 1) * LB)
                pe.wait_ge(b_low_done, n + 1)
                for i in range(LB):
                    wait(pe, x_copied, (n - 1) * LB + i + 1)
                    cols = slice(i * P, (i + 1) * P)
                    terms = [(at_low, b_high, j) for j in range(LB)]
                    terms += [(at_high, part, j) for j in range(LB) for part in (b_low, b_high)]
                    for k, (left, right, j) in enumerate(terms):
                        last = pe.matmul(ps_x[i][:, 0:L], left[d % 2][:, j, cols], right[d % 2][:, j],
                                         start=k == 0, stop=k == len(terms) - 1)
                    last.then_inc(x_multiplied, 1)

            def body(it, last):
                for d in range(ring):
                    if exists(d + 1, last):
                        transpose(it, d + 1)
                    multiply(it, d)

            transpose(0, 0)
            run(pe, body)


def finish(nc, z_flat, x_dram, out_flat, const):
    z_view = z_flat.rearrange("(n t p) c -> n p t c", p=P, t=CT)
    out_view = out_flat.rearrange("(n t p) c -> n p t c", p=P, t=CT)
    factor_ops = MOMENT_STEPS + 2

    with ExitStack() as ctx:
        def sb(name, shape, dt=F32):
            return ctx.enter_context(nc.sbuf_tensor(name, shape, dt))

        def sbs(name, shape, n):
            return [sb(f"{name}{k}", shape) for k in range(n)]

        def ps(name):
            return ctx.enter_context(nc.psum_tensor(name, [P, 512], F32))

        def sem(name):
            return ctx.enter_context(nc.semaphore(name))

        z = sbs("fz", [P, CT, D], CRING)
        xt = sbs("fxt", [D, CR * L], CRING)
        s_sum = sbs("s_sum", [P, CT, D], CRING)
        result = sbs("result", [P, CT, D], CRING)
        rstd_zc = sbs("rstd_zc", [P, CT], CRING)
        stats = sbs("fstats", [P, 2, CT, 6], CRING)
        work = [[sb(f"fwork{k}_{n}", [P, 2, CT]) for n in range(3)] for k in range(CRING)]
        std = sbs("std", [P, 2, CT], CRING)
        rstd = sbs("frstd", [P, 2, CT], CRING)
        shift = sbs("fshift", [P, 2, CT], CRING)
        eps = sb("eps", [P, 1])
        zt = sbs("fzt", [D, L], 2)
        gate_arg = sbs("gate_arg", [P, L], 2)
        gate0 = sbs("gate0_", [P, L], 2)
        proj = sbs("proj", [P, L], 2)
        y_part = sbs("y_part", [P, L], 2)
        y = sbs("y", [P, L], 2)
        y_biased = sbs("y_biased", [P, L], 4)
        yt = sbs("yt", [D, L], 2)
        row_sum = sbs("row_sum", [D, 1], 2)
        right = sbs("right", [D, 1], 2)
        gate1 = sbs("gate1_", [D, L], 2)
        mixed = sbs("mixed", [D, L], 2)
        w_out = sbs("w_out", [D, D], 2)
        normal = sbs("normal", [P, L], 2)
        scaled = sbs("lnscaled", [P, L], 2)
        ps_z, ps_xn, ps_p, ps_q, ps_y, ps_g, ps_l, ps_o = (
            ps(f"ps_{n}") for n in ("z", "xn", "p", "q", "y", "g", "l", "o"))

        z_loaded = [sem(f"fz_loaded{k}") for k in range(CRING)]
        x_loaded = [sem(f"fx_loaded{k}") for k in range(CRING)]
        stored = [sem(f"out_stored{k}") for k in range(CRING)]
        z_transposed = sem("z_transposed")
        z_copied = sem("z_copied")
        x_transposed = sem("x_transposed")
        p_ready = sem("p_ready")
        q_ready = sem("q_ready")
        arg_ready = sem("arg_ready")
        gate0_ready = sem("gate0_ready")
        proj_ready = sem("proj_ready")
        y_part_ready = sem("y_part_ready")
        y_ready = sem("y_ready")
        y_biased_ready = sem("y_biased_ready")
        y_transposed = sem("y_transposed")
        y_copied = sem("y_copied")
        gate1_in_ready = sem("gate1_in_ready")
        left_ready = sem("left_ready")
        gate1_ready = sem("gate1_ready")
        right_ready = sem("right_ready")
        w_out_ready = sem("w_out_ready")
        mixed_ready = sem("mixed_ready")
        out_ready = sem("out_ready")
        summed = sem("summed")
        normal_ready = sem("normal_ready")
        scaled_ready = sem("scaled_ready")
        result_ready = sem("result_ready")
        x_measured = sem("x_measured")
        s_measured = sem("s_measured")
        factor_steps = sem("ffactor_steps")
        std_ready = sem("std_ready")
        eps_filled = sem("eps_filled")
        rstd_zc_ready = sem("rstd_zc_ready")
        block = ctx.enter_context(nc.Block())
        bodies = L // BODY_R

        def run(engine, step):
            for r in range(BODY_R):
                step(0, r)
            with engine.Fori(1, bodies - 1) as it:
                for r in range(BODY_R):
                    step(it, r)
            for r in range(BODY_R + NORM_BEHIND):
                step(bodies - 1, r)

        def exists(it, r):
            return not isinstance(it, int) or 0 <= it * BODY_R + r < L

        def chunk_slot(r):
            return (r // CR) % CRING

        def halves(it, c):
            if not isinstance(it, int):
                return slice(0, 2)
            n = it * CRING + c
            return slice(0 if n + 1 < CHUNKS else 1, 2 if n >= 1 else 1)

        def pair_exists(it, c):
            return not isinstance(it, int) or it * CRING + c <= CHUNKS

        def dma_count(it, r):
            return (it + (r // CR) // CRING + 1) * 16

        @block.sync
        def _(sp):
            def load(it, c):
                rows = it * BODY_R + (c - CRING + 1) * CR
                wait(sp, y_ready, rows)
                sp.dma_start(z[c % CRING][:], z_view[it * CRING + c]).then_inc(z_loaded[c % CRING], 16)
                wait(sp, q_ready, rows)
                sp.dma_start(xt[c % CRING][:], x_dram[:, bass.ds((it * CRING + c) * CR * L, CR * L)])\
                    .then_inc(x_loaded[c % CRING], 16)

            def store(it, c):
                sp.wait_ge(result_ready, it * BODY_R + (c + 1) * CR)
                sp.dma_start(out_view[it * CRING + c], result[c % CRING][:])\
                    .then_inc(stored[c % CRING], 16)

            def body(it, first, last):
                for c in range(CRING):
                    if not last:
                        load(it, c + CRING)
                    if not (first and c == 0):
                        store(it, c - 1)

            for c in range(CRING):
                load(0, c)
            body(0, True, False)
            with sp.Fori(1, bodies - 1) as it:
                body(it, False, False)
            body(bodies - 1, False, True)
            store(bodies - 1, CRING - 1)
            for k in range(CRING):
                sp.wait_ge(stored[k], 16 * bodies)

        @block.tensor
        def _(pe):
            ident = const["identity"]

            def transpose_y(it, r):
                n = it * BODY_R + r
                pe.wait_ge(y_ready, n + 1)
                wait(pe, y_copied, n)
                for t in range(LB):
                    last = pe.transpose(ps_y[:, t * P:(t + 1) * P], y[r % 2][:, t * D:(t + 1) * D], ident[:])
                last.then_inc(y_transposed, 1)

            def transpose_z(it, r):
                n = it * BODY_R + r
                if r % CR == 0:
                    pe.wait_ge(z_loaded[chunk_slot(r)], dma_count(it, r))
                wait(pe, z_copied, n)
                for t in range(LB):
                    last = pe.transpose(ps_z[:, t * P:(t + 1) * P],
                                        z[chunk_slot(r)][:, (r % CR) * LB + t], ident[:])
                last.then_inc(z_transposed, 1)

            def transpose_x(it, r):
                n = it * BODY_R + r
                if r % CR == 0:
                    pe.wait_ge(x_loaded[chunk_slot(r)], dma_count(it, r))
                wait(pe, x_measured, n)
                for t in range(LB):
                    at = (r % CR) * L + t * P
                    last = pe.transpose(ps_xn[:, t * P:(t + 1) * P], xt[chunk_slot(r)][:, at:at + P], ident[:])
                last.then_inc(x_transposed, 1)

            def project_z(it, r):
                n = it * BODY_R + r
                pe.wait_ge(z_copied, n + 1)
                wait(pe, arg_ready, n)
                for t in range(LB):
                    last = pe.matmul(ps_p[:, t * D:(t + 1) * D], zt[r % 2][:, t * P:(t + 1) * P],
                                     const["Wgo"][:], start=True, stop=True)
                last.then_inc(p_ready, 1)

            def project_x(it, r):
                n = it * BODY_R + r
                wait(pe, proj_ready, n)
                for t in range(LB):
                    at = (r % CR) * L + t * P
                    last = pe.matmul(ps_q[:, t * D:(t + 1) * D], xt[chunk_slot(r)][:, at:at + P],
                                     const["Wo"][:], start=True, stop=True)
                last.then_inc(q_ready, 1)

            def multiply_y(it, r):
                n = it * BODY_R + r
                pe.wait_ge(y_copied, n + 1)
                wait(pe, gate1_ready, n)
                pe.matmul(ps_g[:, 0:L], const["Wg"][:], yt[r % 2][:], start=True, stop=True)\
                    .then_inc(gate1_in_ready, 1)
                wait(pe, mixed_ready, n)
                wait(pe, right_ready, n)
                pe.matmul(ps_l[:, L:L + 1], const["Wr"][:], row_sum[r % 2][:], start=True, stop=True)
                pe.matmul(ps_l[:, 0:L], const["Wle"][:], yt[r % 2][:], start=True, stop=True)\
                    .then_inc(left_ready, 1)

            def multiply_out(it, r):
                n = it * BODY_R + r
                pe.wait_ge(mixed_ready, n + 1)
                pe.wait_ge(w_out_ready, n + 1)
                wait(pe, summed, n)
                for t in range(LB):
                    last = pe.matmul(ps_o[:, t * D:(t + 1) * D], mixed[r % 2][:, t * P:(t + 1) * P],
                                     w_out[r % 2][:], start=True, stop=True)
                last.then_inc(out_ready, 1)

            def step(it, r):
                for part, row in ((transpose_y, r - 1), (transpose_z, r + 1), (project_z, r),
                                  (project_x, r), (multiply_y, r - 1), (multiply_out, r - 2),
                                  (transpose_x, r + X_AHEAD)):
                    if exists(it, row):
                        part(it, row)

            transpose_z(0, 0)
            for r in range(X_AHEAD):
                transpose_x(0, r)
            run(pe, step)

        @block.scalar
        def _(act):
            def copy_y(it, r):
                n = it * BODY_R + r
                act.wait_ge(y_transposed, n + 1)
                wait(act, left_ready, n - 1)
                act.activation(yt[r % 2][:], ps_y[:, 0:L], ACT.Identity, accum_out=row_sum[r % 2][:])\
                    .then_inc(y_copied, 1)

            def copy_z(it, r):
                n = it * BODY_R + r
                act.wait_ge(z_transposed, n + 1)
                wait(act, p_ready, n - 1)
                act.activation(zt[r % 2][:], ps_z[:, 0:L], ACT.Identity).then_inc(z_copied, 1)

            def sigmoid0(it, r):
                n = it * BODY_R + r
                act.wait_ge(arg_ready, n + 1)
                wait(act, y_part_ready, n - 1)
                act.activation(gate0[r % 2][:], gate_arg[r % 2][:], ACT.Sigmoid).then_inc(gate0_ready, 1)

            def sigmoid1(it, r):
                n = it * BODY_R + r
                act.wait_ge(gate1_in_ready, n + 1)
                wait(act, mixed_ready, n - 1)
                act.activation(gate1[r % 2][:], ps_g[:, 0:L], ACT.Sigmoid, bias=const["bg"][:, 0:1])\
                    .then_inc(gate1_ready, 1)

            def scale_w_out(it, r):
                n = it * BODY_R + r
                act.wait_ge(right_ready, n + 1)
                wait(act, out_ready, n - 1)
                act.activation(w_out[r % 2][:], const["Wout"][:], ACT.Identity, scale=right[r % 2][:, 0:1])\
                    .then_inc(w_out_ready, 1)

            def normalise(it, r):
                n = it * BODY_R + r
                k = chunk_slot(r)
                if r % CR == 0:
                    act.wait_ge(factor_steps, (it * CRING + r // CR + 3) * factor_ops)
                wait(act, scaled_ready, n - 1)
                for t in range(LB):
                    m = (r % CR) * LB + t
                    pair = (k + 1) % CRING
                    last = act.activation(normal[r % 2][:, t * D:(t + 1) * D], s_sum[k][:, m], ACT.Identity,
                                          bias=shift[pair][:, 1, m:m + 1], scale=rstd[pair][:, 1, m:m + 1])
                last.then_inc(normal_ready, 1)

            def deviation(it, c):
                h = halves(it, c)
                act.wait_ge(factor_steps, (it * CRING + c + 1) * factor_ops + MOMENT_STEPS)
                act.activation(std[c % CRING][:, h], work[c % CRING][1][:, h], ACT.Sqrt,
                               bias=eps[:, 0:1], scale=1.0 / D).then_inc(std_ready, 1)

            def step(it, r):
                for part, row in ((copy_y, r - 1), (copy_z, r + 1), (sigmoid0, r), (sigmoid1, r - 1)):
                    if exists(it, row):
                        part(it, row)
                if r % CR == 2 and pair_exists(it, r // CR):
                    deviation(it, r // CR)
                for part, row in ((scale_w_out, r - 1), (normalise, r - NORM_BEHIND)):
                    if exists(it, row):
                        part(it, row)

            act.wait_ge(eps_filled, 1)
            deviation(0, -1)
            copy_z(0, 0)
            run(act, step)

        @block.vector
        def _(dve):
            def measure_x(it, r):
                n = it * BODY_R + r
                k = chunk_slot(r)
                dve.wait_ge(x_transposed, n + 1)
                for t in range(LB):
                    last = dve.bn_stats(stats[(k - 1) % CRING][:, 0, (r % CR) * LB + t],
                                        ps_xn[:, t * P:(t + 1) * P])
                last.then_inc(x_measured, 1)

            def pair_moments(it, c):
                h = halves(it, c)
                k = c % CRING
                if h.start == 0:
                    dve.wait_ge(x_measured, it * BODY_R + (c + 2) * CR)
                if h.stop == 2:
                    dve.wait_ge(s_measured, it * BODY_R + c * CR)
                moments(dve, stats[k][:, h], [x[:, h] for x in work[k]], factor_steps,
                        (it * CRING + c + 1) * factor_ops)

            def pair_factors(it, c):
                h = halves(it, c)
                k = c % CRING
                base = (it * CRING + c + 1) * factor_ops + MOMENT_STEPS
                dve.wait_ge(std_ready, it * CRING + c + 2)
                if h.stop == 2:
                    wait(dve, normal_ready, it * BODY_R + (c - CRING) * CR)
                dve.reciprocal(rstd[k][:, h], std[k][:, h]).then_inc(factor_steps, 1)
                dve.wait_ge(factor_steps, base + 1)
                dve.scalar_tensor_tensor(shift[k][:, h], work[k][0][:, h], -0.5, rstd[k][:, h],
                                         ALU.mult, ALU.mult).then_inc(factor_steps, 1)
                if h.start == 0:
                    n = it * CRING + c + 1
                    dve.tensor_copy(rstd_zc[k][:], const["rstd_z"][:, bass.ds(n * CT, CT)])\
                        .then_inc(rstd_zc_ready, 1)

            def add_bias(it, r, bank, factor, bias, to, done):
                for t in range(LB):
                    m = (r % CR) * LB + t
                    last = dve.scalar_tensor_tensor(
                        to[r % 2][:, t * D:(t + 1) * D], bank[:, t * D:(t + 1) * D],
                        factor[:, m:m + 1], bias[:], ALU.mult, ALU.add)
                last.then_inc(done, 1)

            def gate_argument(it, r):
                n = it * BODY_R + r
                if r % CR == 0:
                    dve.wait_ge(rstd_zc_ready, it * CRING + r // CR + 1)
                dve.wait_ge(p_ready, n + 1)
                wait(dve, gate0_ready, n - 1)
                add_bias(it, r, ps_p, rstd_zc[(chunk_slot(r) - 1) % CRING], const["bgo"], gate_arg, arg_ready)

            def projection(it, r):
                n = it * BODY_R + r
                if r % CR == 0:
                    dve.wait_ge(factor_steps, (it * CRING + r // CR + 1) * factor_ops)
                dve.wait_ge(q_ready, n + 1)
                wait(dve, y_part_ready, n - 1)
                add_bias(it, r, ps_q, rstd[(chunk_slot(r) - 1) % CRING][:, 0], const["bo"], proj, proj_ready)

            def mix(it, r):
                n = it * BODY_R + r
                dve.wait_ge(left_ready, n + 1)
                wait(dve, w_out_ready, n - 1)
                dve.tensor_tensor(right[r % 2][:], ps_l[:, L:L + 1], const["br"][:], ALU.add)\
                    .then_inc(right_ready, 1)
                dve.wait_ge(gate1_ready, n + 1)
                wait(dve, out_ready, n - 1)
                dve.scalar_tensor_tensor(mixed[r % 2][:], ps_l[:, 0:L], const["ble"][:, 0:1],
                                         gate1[r % 2][:], ALU.add, ALU.mult).then_inc(mixed_ready, 1)

            def add_residual(it, r):
                n = it * BODY_R + r
                k = chunk_slot(r)
                dve.wait_ge(out_ready, n + 1)
                dve.wait_ge(y_biased_ready, n + 1)
                if r % CR == 0:
                    wait(dve, normal_ready, n - (CRING - 1) * CR)
                m = (r % CR) * LB
                dve.tensor_tensor(s_sum[k][:, m:m + LB].rearrange("p t c -> p (t c)"), ps_o[:, 0:L],
                                  y_biased[r % 4][:], ALU.add).then_inc(summed, 1)

            def measure_s(it, r):
                n = it * BODY_R + r
                k = chunk_slot(r)
                dve.wait_ge(summed, n + 1)
                for t in range(LB):
                    m = (r % CR) * LB + t
                    last = dve.bn_stats(stats[(k + 1) % CRING][:, 1, m], s_sum[k][:, m])
                last.then_inc(s_measured, 1)

            def step(it, r):
                for part, row in ((gate_argument, r), (projection, r), (mix, r - 1),
                                  (add_residual, r - 2), (measure_x, r + X_AHEAD), (measure_s, r - 2)):
                    if exists(it, row):
                        part(it, row)
                if r % CR == 1 and pair_exists(it, r // CR):
                    pair_moments(it, r // CR)
                if r % CR == 2 and pair_exists(it, r // CR):
                    pair_factors(it, r // CR)

            dve.memset(eps[:], EPS).then_inc(eps_filled, 1)
            for r in range(X_AHEAD):
                measure_x(0, r)
                if r == CR - 1:
                    pair_moments(0, -1)
            pair_factors(0, -1)
            run(dve, step)

        @block.gpsimd
        def _(pool):
            def residual0(it, r):
                n = it * BODY_R + r
                pool.wait_ge(proj_ready, n + 1)
                pool.wait_ge(gate0_ready, n + 1)
                pool.tensor_tensor(y_part[r % 2][:], proj[r % 2][:], gate0[r % 2][:],
                                          ALU.mult).then_inc(y_part_ready, 1)
                wait(pool, y_transposed, n - 1)
                pool.wait_ge(y_part_ready, n + 1)
                m = (r % CR) * LB
                pool.tensor_tensor(y[r % 2][:], y_part[r % 2][:],
                                   z[chunk_slot(r)][:, m:m + LB].rearrange("p t c -> p (t c)"),
                                   ALU.add).then_inc(y_ready, 1)

            def add_out_bias(it, r):
                n = it * BODY_R + r
                pool.wait_ge(y_ready, n + 1)
                wait(pool, summed, n - 3)
                pool.tensor_tensor(y_biased[r % 4][:], y[r % 2][:], const["bout"][:],
                                          ALU.add).then_inc(y_biased_ready, 1)

            def scale_result(it, r):
                n = it * BODY_R + r
                pool.wait_ge(normal_ready, n + 1)
                pool.tensor_tensor(scaled[r % 2][:], normal[r % 2][:], const["ln_scale"][:],
                                          ALU.mult).then_inc(scaled_ready, 1)

            def shift_result(it, r):
                n = it * BODY_R + r
                k = chunk_slot(r)
                if r % CR == 0:
                    wait(pool, stored[k], dma_count(it, r) - 16)
                pool.wait_ge(scaled_ready, n + 1)
                m = (r % CR) * LB
                pool.tensor_tensor(result[k][:, m:m + LB].rearrange("p t c -> p (t c)"),
                                          scaled[r % 2][:], const["ln_bias"][:],
                                          ALU.add).then_inc(result_ready, 1)

            def step(it, r):
                for part, row in ((residual0, r), (scale_result, r - NORM_BEHIND), (add_out_bias, r),
                                  (shift_result, r - NORM_BEHIND)):
                    if exists(it, row):
                        part(it, row)

            run(pool, step)


_WEIGHTS = {"Wa": ("L0_conv_Wa", True), "Wga": ("L0_conv_Wga", True), "Wb": ("L0_conv_Wb", True),
            "Wgb": ("L0_conv_Wgb", True), "Wo": ("L0_conv_Wo", True), "Wgo": ("L0_conv_Wgo", True),
            "Wl": ("L1_conv_W_left", False), "We": ("L1_conv_W_eq", False),
            "Wr": ("L1_conv_W_right", False), "Wg": ("L1_conv_W_gate", False),
            "Wout": ("L1_conv_W_out", False)}
_VECTORS = {"norm_g": "L0_conv_norm_g", "norm_b": "L0_conv_norm_b", "normo_g": "L0_conv_normo_g",
            "normo_b": "L0_conv_normo_b", "ba": "L0_conv_ba", "bga": "L0_conv_bga", "bb": "L0_conv_bb",
            "bgb": "L0_conv_bgb", "bo": "L0_conv_bo", "bgo": "L0_conv_bgo", "bl": "L1_conv_b_left",
            "be": "L1_conv_b_eq", "br": "L1_conv_b_right", "bg": "L1_conv_b_gate",
            "bout": "L1_conv_b_out", "ln_scale": "L1_conv_ln_scale", "ln_bias": "L1_conv_ln_bias"}


def kernel(**inputs):
    import concourse.bacc as bacc
    import numpy as np
    from concourse.bass_utils import run_bass_kernel_spmd

    nc = bacc.Bacc("TRN2", target_bir_lowering=False, num_devices=1)
    arrays = {}

    def give(name, array):
        array = np.ascontiguousarray(array)
        arrays[name] = array
        return nc.dram_tensor(name, array.shape, mybir.dt.from_np(array.dtype), kind="ExternalInput").ap()

    x = give("x_in", np.asarray(inputs["x"]))
    w = {n: give("w_" + n, np.asarray(inputs[k]).T if turned else np.asarray(inputs[k]))
         for n, (k, turned) in _WEIGHTS.items()}
    vec = {n: give("v_" + n, np.asarray(inputs[k])) for n, k in _VECTORS.items()}
    out = nc.dram_tensor("out", (1, L, L, D), F32, kind="ExternalOutput").ap()
    bass_pair_layers(nc, x, w, vec, out)
    r = run_bass_kernel_spmd(nc, [arrays], core_ids=[0])
    return r.results[0]["out"]
```

```python
from contextlib import ExitStack

import concourse.bass as bass
from concourse import mybir

F32 = mybir.dt.float32
F32R = mybir.dt.float32r
I32 = mybir.dt.int32
ALU = mybir.AluOpType
ACT = mybir.ActivationFunctionType

P = 128
D = 128
L = 384
LB = L // P
TOKENS = L * L
EPS = 1e-5

GT = 4
GROUP = GT * P
GROUPS = TOKENS // GROUP
LOAD_G = 2
LOAD_RING = 6
BATCH_G = 4
BODY_G = 12
BATCH_RING = BODY_G // BATCH_G
STATS_AHEAD = 8
NORM_POOL = 3

CR = 4
CT = CR * LB
CHUNKS = L // CR
CRING = 3
BODY_R = CR * CRING
TO_SUM = 4
TO_NORM = 10
TO_RESULT = 11


def wait(engine, semaphore, value):
    if isinstance(value, int) and value <= 0:
        return
    engine.wait_ge(semaphore, value)


MOMENT_STEPS = 5

RSQRT_BITS = float(0x5F3759DF)
NEWTON_STEPS = 3


def moments(dve, stats, work, steps, base):
    double_mean, total, square = work
    dve.tensor_tensor(double_mean, stats[..., 1], stats[..., 4], ALU.subtract).then_inc(steps, 1)
    dve.tensor_tensor(total, stats[..., 2], stats[..., 5], ALU.add).then_inc(steps, 1)
    dve.wait_ge(steps, base + 1)
    dve.scalar_tensor_tensor(square, double_mean, D / 4.0, double_mean, ALU.mult, ALU.mult)\
        .then_inc(steps, 1)
    dve.wait_ge(steps, base + 3)
    dve.tensor_tensor(total, total, square, ALU.add).then_inc(steps, 1)
    dve.tensor_tensor(double_mean, stats[..., 1], stats[..., 4], ALU.add).then_inc(steps, 1)


def bass_pair_layers(nc, x, w, vec, out):
    a_dram = nc.dram_tensor("a_scratch", (D, TOKENS), F32, kind="Internal").ap()
    b_dram = nc.dram_tensor("b_scratch", (D, TOKENS), F32, kind="Internal").ap()
    x_dram = nc.dram_tensor("x_scratch", (D, TOKENS), F32, kind="Internal").ap()
    z_flat = x.rearrange("b i j c -> (b i j) c")
    out_flat = out.rearrange("b i j c -> (b i j) c")

    with ExitStack() as ctx:
        def sb(name, shape, dt=F32):
            return ctx.enter_context(nc.sbuf_tensor(name, shape, dt))

        const = {
            "identity": sb("identity", [P, P]),
            "rstd": sb("rstd_zx", [P, 2, TOKENS // P]),
        }
        for n in ("Wa", "Wga", "Wb", "Wgb"):
            const[n + "_high"] = sb(n + "_high", [D, D], F32R)
            const[n + "_low"] = sb(n + "_low", [D, D], F32R)
        for n in ("Wgo", "Wo", "Wle", "Wg", "Wr", "Wout"):
            const[n] = sb(n + "_c", [D, D])
        for n in ("ba", "bga", "bb", "bgb", "ble", "bg", "br"):
            const[n] = sb(n + "_col", [D, 1])
        for n in ("bgo", "bo"):
            const[n] = sb(n + "_row", [P, D])
        for n in ("bout", "ln_scale", "ln_bias"):
            const[n] = sb(n + "_row", [P, LB * D])

        prepare(nc, w, vec, const)
        project(nc, z_flat, a_dram, b_dram, const)
        triangle(nc, a_dram, b_dram, x_dram, const)
        finish(nc, z_flat, x_dram, out_flat, const)


def prepare(nc, w, vec, const):
    with ExitStack() as ctx:
        def sb(name, shape, dt=F32):
            return ctx.enter_context(nc.sbuf_tensor(name, shape, dt))

        def sem(name):
            return ctx.enter_context(nc.semaphore(name))

        gated = ("Wa", "Wga", "Wb", "Wgb")
        raw = {n: sb("raw_" + n, [D, D]) for n in (*gated, "Wgo", "Wo", "Wl", "We")}
        scaled = {n: sb("scaled_" + n, [D, D]) for n in (*gated, "Wgo", "Wo")}
        col = {n: sb("col_" + n, [D, 1]) for n in
               ("norm_g", "norm_b", "normo_g", "normo_b", "ba", "bga", "bb", "bgb", "bl", "be", "br")}
        row = {n: sb("row_" + n, [P, D]) for n in ("bgo", "bo")}
        spread = {n: sb("spread_" + n, [D, P]) for n in ("norm_b", "normo_b")}
        ones = sb("ones", [D, P])
        inv_d = sb("inv_d", [D, P])
        psum_col = ctx.enter_context(nc.psum_tensor("prep_col", [D, 4], F32))
        psum_row = [ctx.enter_context(nc.psum_tensor(f"prep_row{k}", [P, D], F32)) for k in range(2)]
        psum_mean = [ctx.enter_context(nc.psum_tensor(f"prep_mean{k}", [P, D], F32)) for k in range(2)]

        loaded = sem("prep_loaded")
        filled = sem("prep_filled")
        chain = sem("prep_chain")
        multiplied = sem("prep_multiplied")
        block = ctx.enter_context(nc.Block())

        def column(v):
            return v.rearrange("(c o) -> c o", o=1)

        def spread_row(v):
            return v.rearrange("(o c) -> o c", o=1).partition_broadcast(P)

        loads = [(raw[n][:], w[n]) for n in raw]
        loads += [(const[n][:], w[n]) for n in ("Wg", "Wr", "Wout")]
        loads += [(col[n][:], column(vec[n])) for n in col]
        loads += [(const["bg"][:], column(vec["bg"]))]
        loads += [(row[n][:], spread_row(vec[n])) for n in row]
        loads += [(const[n][:, k * D:(k + 1) * D], spread_row(vec[n]))
                  for n in ("bout", "ln_scale", "ln_bias") for k in range(LB)]

        @block.sync
        def _(sp):
            for to, of in loads:
                sp.dma_start(to, of).then_inc(loaded, 16)

        @block.gpsimd
        def _(pool):
            pool.memset(const["identity"][:], 0.0).then_inc(filled, 1)
            pool.wait_ge(filled, 1)
            pool.affine_select(out=const["identity"][:], in_=const["identity"][:],
                               compare_op=ALU.not_equal, fill=1.0, base=0,
                               pattern=[[-1, P]], channel_multiplier=1).then_inc(filled, 1)

        @block.vector
        def _(dve):
            count = [0]

            def step(ins):
                ins.then_inc(chain, 1)
                count[0] += 1

            def settle():
                dve.wait_ge(chain, count[0])

            step(dve.memset(ones[:], 1.0))
            step(dve.memset(inv_d[:], 1.0 / D))
            settle()
            dve.wait_ge(loaded, 16 * len(loads))
            for n, v in (("norm_b", "norm_b"), ("normo_b", "normo_b")):
                step(dve.tensor_scalar(spread[n][:], ones[:], col[v][:, 0:1], None, ALU.mult))
            for n in (*gated, "Wgo"):
                step(dve.tensor_scalar(scaled[n][:], raw[n][:], col["norm_g"][:, 0:1], None, ALU.mult))
            step(dve.tensor_scalar(scaled["Wo"][:], raw["Wo"][:], col["normo_g"][:, 0:1], None, ALU.mult))
            step(dve.tensor_tensor(const["Wle"][:], raw["Wl"][:], raw["We"][:], ALU.add))
            step(dve.tensor_tensor(const["ble"][:], col["bl"][:], col["be"][:], ALU.add))
            step(dve.tensor_scalar(const["br"][:], col["br"][:], float(L), None, ALU.mult))
            settle()
            assert count[0] == SCALED
            for n in gated:
                step(dve.tensor_copy(const[n + "_high"][:], scaled[n][:]))
            settle()
            for n in gated:
                step(dve.tensor_tensor(const[n + "_low"][:], scaled[n][:],
                                       const[n + "_high"][:].bitcast(F32), ALU.subtract))
            dve.wait_ge(multiplied, 8)
            for k, n in enumerate(("ba", "bga", "bb", "bgb")):
                step(dve.tensor_tensor(const[n][:], psum_col[:, k:k + 1], col[n][:], ALU.add))
            for k, n in enumerate(("bgo", "bo")):
                step(dve.tensor_tensor(const[n][:], psum_row[k][:], row[n][:], ALU.add))
            for k, n in enumerate(("Wgo", "Wo")):
                step(dve.tensor_tensor(const[n][:], scaled[n][:], psum_mean[k][:], ALU.subtract))
            settle()

        @block.tensor
        def _(pe):
            pe.wait_ge(loaded, 16 * len(loads))
            pe.wait_ge(chain, SCALED)
            for k, n in enumerate(gated):
                pe.matmul(psum_col[:, k:k + 1], raw[n][:], col["norm_b"][:], start=True, stop=True)\
                    .then_inc(multiplied, 1)
            for k, (n, v) in enumerate((("Wgo", "norm_b"), ("Wo", "normo_b"))):
                pe.matmul(psum_row[k][:], spread[v][:], raw[n][:], start=True, stop=True)\
                    .then_inc(multiplied, 1)
                pe.matmul(psum_mean[k][:], inv_d[:], scaled[n][:], start=True, stop=True)\
                    .then_inc(multiplied, 1)


SCALED = 2 + 2 + 5 + 1 + 3


def project(nc, z_flat, a_dram, b_dram, const):
    z_view = z_flat.rearrange("(n t p) c -> n p t c", p=P, t=LOAD_G * GT)
    batch = BATCH_G * GROUP
    tiles = BATCH_G * GT
    stats_ops = tiles + MOMENT_STEPS + 2
    factor_ops = 3

    with ExitStack() as ctx:
        def sb(name, shape, dt=F32):
            return ctx.enter_context(nc.sbuf_tensor(name, shape, dt))

        def ps(name):
            return ctx.enter_context(nc.psum_tensor(name, [P, GROUP], F32))

        def sem(name):
            return ctx.enter_context(nc.semaphore(name))

        z = [sb(f"z{k}", [P, LOAD_G * GT, D]) for k in range(LOAD_RING)]
        stats = [sb(f"stats{k}", [P, tiles, 6]) for k in range(BATCH_RING)]
        work = [[sb(f"stats_work{k}_{n}", [P, tiles]) for n in range(3)] for k in range(BATCH_RING)]
        power = sb("power", [P, tiles])
        rstd = [sb(f"rstd{k}", [P, tiles]) for k in range(BATCH_RING)]
        shift = [sb(f"shift{k}", [P, tiles]) for k in range(BATCH_RING)]
        zn = [sb(f"zn{k}", [P, GROUP]) for k in range(4)]
        zt_high = [sb(f"zt_high{k}", [D, GROUP], F32R) for k in range(2)]
        zt_low = [sb(f"zt_low{k}", [D, GROUP], F32R) for k in range(2)]
        gate = [sb(f"gate{k}", [D, GROUP]) for k in range(2)]
        gated_out = [[sb(f"gated{h}_{k}", [D, batch]) for k in range(BATCH_RING)] for h in range(2)]
        ps_zt = [ps(f"ps_zt{k}") for k in range(2)]
        ps_gate = [ps(f"ps_gate{k}") for k in range(2)]
        ps_lin = [ps(f"ps_lin{k}") for k in range(4)]

        z_loaded = [sem(f"z_loaded{k}") for k in range(LOAD_RING)]
        stats_steps = sem("stats_steps")
        factor_steps = sem("factor_steps")
        power_filled = sem("power_filled")
        normed = sem("normed")
        normed_pool = sem("normed_pool")
        scaled_pool = sem("scaled_pool")
        transposed = sem("transposed")
        high_done = sem("high_done")
        low_done = sem("low_done")
        multiplied = sem("multiplied")
        sigmoid_done = sem("sigmoid_done")
        gated = sem("gated")
        stored = [[sem(f"stored{h}_{k}") for k in range(BATCH_RING)] for h in range(2)]
        block = ctx.enter_context(nc.Block())

        weights = [("Wga", "Wa"), ("Wgb", "Wb")]
        biases = [("bga", "ba"), ("bgb", "bb")]
        loads_per_body = BODY_G // LOAD_G
        batches_per_body = BODY_G // BATCH_G
        bodies = GROUPS // BODY_G

        def run(engine, body):
            body(0, True, False)
            with engine.Fori(1, bodies - 1) as it:
                body(it, False, False)
            body(bodies - 1, False, True)

        def exists(g, last):
            return not last or g < BODY_G

        @block.sync
        def _(sp):
            def load(it, k):
                wait(sp, normed, it * BODY_G + LOAD_G * (k - LOAD_RING + 1))
                wait(sp, normed_pool, it * BODY_G + LOAD_G * (k - LOAD_RING + 1))
                sp.dma_start(z[k % LOAD_RING][:], z_view[it * loads_per_body + k])\
                    .then_inc(z_loaded[k % LOAD_RING], 16)

            def body(it, first, last):
                for j in range(batches_per_body):
                    for k in range(2 * j, 2 * j + 2):
                        if not last:
                            load(it, k + LOAD_RING)
                    for h, to in enumerate((a_dram, b_dram)):
                        sp.wait_ge(gated, it * 2 * BODY_G + 2 * BATCH_G * (j + 1) - 1 + h)
                        sp.dma_start(to[:, bass.ds((it * batches_per_body + j) * batch, batch)],
                                     gated_out[h][j][:]).then_inc(stored[h][j], 16)

            for k in range(LOAD_RING):
                load(0, k)
            run(sp, body)
            for h in range(2):
                for k in range(BATCH_RING):
                    sp.wait_ge(stored[h][k], 16 * bodies)

        @block.vector
        def _(dve):
            def measure(it, g):
                k = g // LOAD_G
                if g % LOAD_G == 0:
                    dve.wait_ge(z_loaded[k % LOAD_RING], (it + k // LOAD_RING + 1) * 16)
                for t in range(GT):
                    dve.bn_stats(stats[(g // BATCH_G) % BATCH_RING][:, (g % BATCH_G) * GT + t, :],
                                 z[k % LOAD_RING][:, (g % LOAD_G) * GT + t, :]).then_inc(stats_steps, 1)

            def close(it, b):
                k = b % BATCH_RING
                base = (it * batches_per_body + b) * stats_ops + tiles
                dve.wait_ge(stats_steps, base)
                wait(dve, factor_steps, (it * batches_per_body + b - BATCH_RING + 1) * factor_ops)
                moments(dve, stats[k][:], [x[:] for x in work[k]], stats_steps, base)
                dve.wait_ge(stats_steps, base + MOMENT_STEPS)
                dve.tensor_scalar(work[k][1][:], work[k][1][:], 1.0 / D, EPS, ALU.mult, ALU.add)\
                    .then_inc(stats_steps, 1)
                dve.tensor_scalar(work[k][0][:], work[k][0][:], -0.5, None, ALU.mult)\
                    .then_inc(stats_steps, 1)

            def low(it, g):
                dve.wait_ge(high_done, it * BODY_G + g + 1)
                dve.tensor_tensor(zt_low[g % 2][:], ps_zt[g % 2][:], zt_high[g % 2][:].bitcast(F32),
                                  ALU.subtract).then_inc(low_done, 1)

            def apply_gate(it, g, h):
                u = 2 * g + h
                if g % BATCH_G == 0:
                    wait(dve, stored[h][g // BATCH_G], 16 * it)
                dve.wait_ge(sigmoid_done, it * 2 * BODY_G + u + 1)
                dve.wait_ge(multiplied, it * 4 * BODY_G + 2 * u + 2)
                at = (g % BATCH_G) * GROUP
                dve.scalar_tensor_tensor(gated_out[h][g // BATCH_G][:, at:at + GROUP],
                                         ps_lin[u % 4][:], const[biases[h][1]][:, 0:1],
                                         gate[u % 2][:], ALU.add, ALU.mult).then_inc(gated, 1)

            def body(it, first, last):
                for g in range(BODY_G):
                    if exists(g + 1, last):
                        low(it, g + 1)
                    if exists(g + STATS_AHEAD, last):
                        measure(it, g + STATS_AHEAD)
                        if (g + STATS_AHEAD) % BATCH_G == BATCH_G - 1:
                            close(it, (g + STATS_AHEAD) // BATCH_G)
                    for h in range(2):
                        apply_gate(it, g, h)

            for g in range(STATS_AHEAD):
                measure(0, g)
                if g % BATCH_G == BATCH_G - 1:
                    close(0, g // BATCH_G)
            low(0, 0)
            run(dve, body)

        @block.scalar
        def _(act):
            def normalise(it, g):
                b = g // BATCH_G
                if g % BATCH_G == 0:
                    act.wait_ge(factor_steps, (it * batches_per_body + b) * factor_ops + 2)
                wait(act, transposed, it * BODY_G + g - 3)
                tiles_here = [t for t in range(GT) if t != NORM_POOL]
                for t in tiles_here:
                    n = (g % BATCH_G) * GT + t
                    last = act.activation(zn[g % 4][:, t * D:(t + 1) * D],
                                          z[(g // LOAD_G) % LOAD_RING][:, (g % LOAD_G) * GT + t, :],
                                          ACT.Identity, bias=shift[b % BATCH_RING][:, n:n + 1],
                                          scale=rstd[b % BATCH_RING][:, n:n + 1])
                last.then_inc(normed, 1)

            def high(it, g):
                act.wait_ge(transposed, it * BODY_G + g + 1)
                wait(act, multiplied, it * 4 * BODY_G + 4 * (g - 1))
                act.activation(zt_high[g % 2][:], ps_zt[g % 2][:], ACT.Identity).then_inc(high_done, 1)

            def sigmoid(it, g, h):
                u = 2 * g + h
                act.wait_ge(multiplied, it * 4 * BODY_G + 2 * u + 1)
                wait(act, gated, it * 2 * BODY_G + u - 1)
                act.activation(gate[u % 2][:], ps_gate[u % 2][:], ACT.Sigmoid,
                               bias=const[biases[h][0]][:, 0:1]).then_inc(sigmoid_done, 1)

            def body(it, first, last):
                for g in range(BODY_G):
                    if exists(g + 1, last):
                        high(it, g + 1)
                    if exists(g + 2, last):
                        normalise(it, g + 2)
                    for h in range(2):
                        sigmoid(it, g, h)

            normalise(0, 0)
            normalise(0, 1)
            high(0, 0)
            run(act, body)

        @block.gpsimd
        def _(pool):
            def factors(it, b):
                k = b % BATCH_RING
                n = it * batches_per_body + b
                pool.wait_ge(stats_steps, (n + 1) * stats_ops)
                wait(pool, normed, it * BODY_G + BATCH_G * (b - BATCH_RING + 1))
                wait(pool, normed_pool, it * BODY_G + BATCH_G * (b - BATCH_RING + 1))
                pool.tensor_tensor(rstd[k][:], work[k][1][:], power[:], ALU.pow).then_inc(factor_steps, 1)
                pool.wait_ge(factor_steps, n * factor_ops + 1)
                pool.tensor_tensor(shift[k][:], work[k][0][:], rstd[k][:], ALU.mult).then_inc(factor_steps, 1)
                pool.tensor_copy(const["rstd"][:, 0, bass.ds(n * tiles, tiles)], rstd[k][:])\
                    .then_inc(factor_steps, 1)

            def normalise(it, g):
                b = g // BATCH_G
                if g % BATCH_G == 0:
                    pool.wait_ge(factor_steps, (it * batches_per_body + b) * factor_ops + 2)
                wait(pool, transposed, it * BODY_G + g - 3)
                t = NORM_POOL
                n = (g % BATCH_G) * GT + t
                to = zn[g % 4][:, t * D:(t + 1) * D]
                pool.tensor_tensor(to, z[(g // LOAD_G) % LOAD_RING][:, (g % LOAD_G) * GT + t, :],
                                   rstd[b][:, n:n + 1].to_broadcast([P, D]), ALU.mult).then_inc(scaled_pool, 1)
                pool.wait_ge(scaled_pool, it * BODY_G + g + 1)
                pool.tensor_tensor(to, to, shift[b][:, n:n + 1].to_broadcast([P, D]), ALU.add)\
                    .then_inc(normed_pool, 1)

            def body(it, first, last):
                for g in range(BODY_G):
                    if g % BATCH_G == 0:
                        factors(it, g // BATCH_G)
                    normalise(it, g)

            pool.memset(power[:], -0.5).then_inc(power_filled, 1)
            pool.wait_ge(power_filled, 1)
            run(pool, body)

        @block.tensor
        def _(pe):
            def transpose(it, g):
                pe.wait_ge(normed, it * BODY_G + g + 1)
                pe.wait_ge(normed_pool, it * BODY_G + g + 1)
                wait(pe, low_done, it * BODY_G + g - 1)
                for t in range(GT):
                    last = pe.transpose(ps_zt[g % 2][:, t * P:(t + 1) * P], zn[g % 4][:, t * D:(t + 1) * D],
                                        const["identity"][:])
                last.then_inc(transposed, 1)

            def multiply(it, g):
                pe.wait_ge(low_done, it * BODY_G + g + 1)
                for h in range(2):
                    u = 2 * g + h
                    for name, bank, free, count in (
                            (weights[h][0], ps_gate[u % 2], sigmoid_done, u - 1),
                            (weights[h][1], ps_lin[u % 4], gated, u - 3)):
                        wait(pe, free, it * 2 * BODY_G + count)
                        w_high, w_low = const[name + "_high"], const[name + "_low"]
                        pe.matmul(bank[:], w_low[:], zt_high[g % 2][:], start=True, stop=False)
                        pe.matmul(bank[:], w_high[:], zt_low[g % 2][:], start=False, stop=False)
                        pe.matmul(bank[:], w_high[:], zt_high[g % 2][:], start=False, stop=True)\
                            .then_inc(multiplied, 1)

            def body(it, first, last):
                for g in range(BODY_G):
                    if exists(g + 1, last):
                        transpose(it, g + 1)
                    multiply(it, g)

            transpose(0, 0)
            run(pe, body)


def triangle(nc, a_dram, b_dram, x_dram, const):
    a_view = a_dram.rearrange("d (n p j) -> d p n j", p=P, n=LB)
    b_view = b_dram.rearrange("d (n p j) -> d p n j", p=P, n=LB)
    x_view = x_dram.rearrange("d (n p j) -> d p n j", p=P, n=LB)
    ring = 4

    with ExitStack() as ctx:
        def sb(name, shape, dt=F32):
            return ctx.enter_context(nc.sbuf_tensor(name, shape, dt))

        def ps(name):
            return ctx.enter_context(nc.psum_tensor(name, [P, 512], F32))

        def sem(name):
            return ctx.enter_context(nc.semaphore(name))

        a_raw = [sb(f"a_raw{k}", [P, LB, L]) for k in range(ring)]
        b_raw = [sb(f"b_raw{k}", [P, LB, L]) for k in range(ring)]
        at_high = [sb(f"at_high{k}", [P, LB, L], F32R) for k in range(2)]
        at_low = [sb(f"at_low{k}", [P, LB, L], F32R) for k in range(2)]
        b_high = [sb(f"b_high{k}", [P, LB, L], F32R) for k in range(2)]
        b_low = [sb(f"b_low{k}", [P, LB, L], F32R) for k in range(2)]
        x_out = [sb(f"x_out{k}", [P, LB, L]) for k in range(2)]
        x_square = [sb(f"x_square{k}", [P, LB, L]) for k in range(2)]
        x_sum = sb("x_sum", [P, LB, L])
        square_sum = sb("square_sum", [P, LB, L])
        x_var = sb("x_var", [P, LB, L])
        eps = sb("x_eps", [P, 1])
        ps_at = [ps(f"ps_at{k}") for k in range(LB)]
        ps_x = [ps(f"ps_x{k}") for k in range(LB)]

        a_loaded = [sem(f"a_loaded{k}") for k in range(ring)]
        b_loaded = [sem(f"b_loaded{k}") for k in range(ring)]
        a_transposed = sem("a_transposed")
        a_high_done = sem("a_high_done")
        a_low_done = sem("a_low_done")
        x_multiplied = sem("x_multiplied")
        x_copied = sem("x_copied")
        x_squared = sem("x_squared")
        x_summed = sem("x_summed")
        squares_summed = sem("squares_summed")
        sums_cleared = sem("sums_cleared")
        x_factor_steps = sem("x_factor_steps")
        x_std_ready = sem("x_std_ready")
        x_factor_transposed = sem("x_factor_transposed")
        b_high_done = sem("b_high_done")
        b_low_done = sem("b_low_done")
        x_stored = [sem(f"x_stored{k}") for k in range(2)]
        block = ctx.enter_context(nc.Block())
        bodies = D // ring

        def run(engine, body):
            body(0, False)
            with engine.Fori(1, bodies - 1) as it:
                body(it, False)
            body(bodies - 1, True)

        def exists(d, last):
            return not last or d < ring

        @block.sync
        def _(sp):
            def load(it, d):
                wait(sp, a_transposed, (it * ring + d - ring + 1) * LB)
                sp.dma_start(a_raw[d % ring][:], a_view[it * ring + d]).then_inc(a_loaded[d % ring], 16)
                wait(sp, b_low_done, it * ring + d - ring + 1)
                sp.dma_start(b_raw[d % ring][:], b_view[it * ring + d]).then_inc(b_loaded[d % ring], 16)

            def body(it, last):
                for d in range(ring):
                    if exists(d + ring, last):
                        load(it, d + ring)
                    sp.wait_ge(x_copied, (it * ring + d + 1) * LB)
                    sp.dma_start(x_view[it * ring + d], x_out[d % 2][:]).then_inc(x_stored[d % 2], 16)

            for d in range(ring):
                load(0, d)
            run(sp, body)
            for k in range(2):
                sp.wait_ge(x_stored[k], 16 * D // 2)

        @block.vector
        def _(dve):
            def split(it, d):
                n = it * ring + d
                dve.wait_ge(b_loaded[d % ring], (it + d // ring + 1) * 16)
                wait(dve, x_multiplied, (n - 1) * LB)
                dve.tensor_copy(b_high[d % 2][:], b_raw[d % ring][:]).then_inc(b_high_done, 1)
                for j in range(LB):
                    dve.wait_ge(a_high_done, n * LB + j + 1)
                    dve.tensor_tensor(at_low[d % 2][:, j], ps_at[j][:, 0:L],
                                      at_high[d % 2][:, j].bitcast(F32), ALU.subtract)\
                        .then_inc(a_low_done, 1)
                dve.wait_ge(b_high_done, n + 1)
                dve.tensor_tensor(b_low[d % 2][:], b_raw[d % ring][:], b_high[d % 2][:].bitcast(F32),
                                  ALU.subtract).then_inc(b_low_done, 1)

            def body(it, last):
                for d in range(ring):
                    if exists(d + 1, last):
                        split(it, d + 1)

            def x_factors():
                dve.wait_ge(x_summed, D)
                dve.wait_ge(squares_summed, D)
                dve.scalar_tensor_tensor(x_var[:], x_sum[:], -1.0 / D, x_sum[:], ALU.mult, ALU.mult)\
                    .then_inc(x_factor_steps, 1)
                dve.wait_ge(x_factor_steps, 1)
                dve.tensor_tensor(x_var[:], x_var[:], square_sum[:], ALU.add).then_inc(x_factor_steps, 1)
                dve.wait_ge(x_factor_steps, 2)
                dve.tensor_scalar(x_var[:], x_var[:], 0.0, 1.0 / D, ALU.max, ALU.mult)\
                    .then_inc(x_factor_steps, 1)
                dve.wait_ge(x_std_ready, 1)
                dve.reciprocal(x_var[:], x_var[:]).then_inc(x_factor_steps, 1)
                by_block = const["rstd"][:, 1].rearrange("p (i k) -> p k i", k=LB)
                for i in range(LB):
                    dve.wait_ge(x_factor_transposed, i + 1)
                    dve.tensor_copy(by_block[:, :, i * P:(i + 1) * P],
                                    ps_at[i][:, 0:L].rearrange("p (k i) -> p k i", k=LB))\
                        .then_inc(x_factor_steps, 1)
                dve.wait_ge(x_factor_steps, 4 + LB)

            dve.memset(eps[:], EPS).then_inc(sums_cleared, 1)
            split(0, 0)
            run(dve, body)
            x_factors()

        @block.scalar
        def _(act):
            def high(it, d):
                n = it * ring + d
                wait(act, x_multiplied, (n - 1) * LB)
                for j in range(LB):
                    act.wait_ge(a_transposed, n * LB + j + 1)
                    act.activation(at_high[d % 2][:, j], ps_at[j][:, 0:L], ACT.Identity)\
                        .then_inc(a_high_done, 1)

            def copy(it, d):
                n = it * ring + d
                wait(act, x_stored[d % 2], (it * (ring // 2) + d // 2) * 16)
                wait(act, x_summed, n - 1)
                wait(act, squares_summed, n - 1)
                for i in range(LB):
                    act.wait_ge(x_multiplied, n * LB + i + 1)
                    act.activation(x_out[d % 2][:, i], ps_x[i][:, 0:L], ACT.Identity)\
                        .then_inc(x_copied, 1)
                    act.activation(x_square[d % 2][:, i], ps_x[i][:, 0:L], ACT.Square)\
                        .then_inc(x_squared, 1)

            def body(it, last):
                for d in range(ring):
                    if exists(d + 1, last):
                        high(it, d + 1)
                    copy(it, d)

            high(0, 0)
            run(act, body)
            act.wait_ge(sums_cleared, 3)
            act.wait_ge(x_factor_steps, 3)
            act.activation(x_var[:], x_var[:], ACT.Sqrt, bias=eps[:, 0:1]).then_inc(x_std_ready, 1)

        @block.gpsimd
        def _(pool):
            def add(it, d):
                n = it * ring + d
                pool.wait_ge(x_copied, (n + 1) * LB)
                wait(pool, x_summed, n)
                pool.tensor_tensor(x_sum[:], x_sum[:], x_out[d % 2][:], ALU.add).then_inc(x_summed, 1)
                pool.wait_ge(x_squared, (n + 1) * LB)
                wait(pool, squares_summed, n)
                pool.tensor_tensor(square_sum[:], square_sum[:], x_square[d % 2][:], ALU.add)\
                    .then_inc(squares_summed, 1)

            def body(it, last):
                for d in range(ring):
                    add(it, d)

            pool.memset(x_sum[:], 0.0).then_inc(sums_cleared, 1)
            pool.memset(square_sum[:], 0.0).then_inc(sums_cleared, 1)
            pool.wait_ge(sums_cleared, 3)
            run(pool, body)

        @block.tensor
        def _(pe):
            def transpose(it, d):
                n = it * ring + d
                pe.wait_ge(a_loaded[d % ring], (it + d // ring + 1) * 16)
                for j in range(LB):
                    wait(pe, a_low_done, (n - 1) * LB + j + 1)
                    for i in range(LB):
                        last = pe.transpose(ps_at[j][:, i * P:(i + 1) * P],
                                            a_raw[d % ring][:, i, j * P:(j + 1) * P], const["identity"][:])
                    last.then_inc(a_transposed, 1)

            def multiply(it, d):
                n = it * ring + d
                pe.wait_ge(a_low_done, (n + 1) * LB)
                pe.wait_ge(b_low_done, n + 1)
                for i in range(LB):
                    wait(pe, x_copied, (n - 1) * LB + i + 1)
                    wait(pe, x_squared, (n - 1) * LB + i + 1)
                    cols = slice(i * P, (i + 1) * P)
                    terms = [(at_low, b_high, j) for j in range(LB)]
                    terms += [(at_high, part, j) for j in range(LB) for part in (b_low, b_high)]
                    for k, (left, right, j) in enumerate(terms):
                        last = pe.matmul(ps_x[i][:, 0:L], left[d % 2][:, j, cols], right[d % 2][:, j],
                                         start=k == 0, stop=k == len(terms) - 1)
                    last.then_inc(x_multiplied, 1)

            def body(it, last):
                for d in range(ring):
                    if exists(d + 1, last):
                        transpose(it, d + 1)
                    multiply(it, d)

            def transpose_factors():
                pe.wait_ge(x_factor_steps, 4)
                for i in range(LB):
                    for k in range(LB):
                        last = pe.transpose(ps_at[i][:, k * P:(k + 1) * P],
                                            x_var[:, i, k * P:(k + 1) * P], const["identity"][:])
                    last.then_inc(x_factor_transposed, 1)

            transpose(0, 0)
            run(pe, body)
            transpose_factors()


def finish(nc, z_flat, x_dram, out_flat, const):
    z_view = z_flat.rearrange("(n t p) c -> n p t c", p=P, t=CT)
    out_view = out_flat.rearrange("(n t p) c -> n p t c", p=P, t=CT)
    refine_steps = 2 + 3 * NEWTON_STEPS + 1
    factor_ops = MOMENT_STEPS + refine_steps

    with ExitStack() as ctx:
        def sb(name, shape, dt=F32):
            return ctx.enter_context(nc.sbuf_tensor(name, shape, dt))

        def sbs(name, shape, n):
            return [sb(f"{name}{k}", shape) for k in range(n)]

        def ps(name):
            return ctx.enter_context(nc.psum_tensor(name, [P, 512], F32))

        def sem(name):
            return ctx.enter_context(nc.semaphore(name))

        z = sbs("fz", [P, CT, D], CRING)
        xt = sbs("fxt", [D, CR * L], CRING)
        s_sum = sbs("s_sum", [P, CT, D], CRING)
        result = sbs("result", [P, CT, D], CRING)
        rstd_zx = sbs("rstd_zx_chunk", [P, 2, CT], CRING)
        stats = sbs("fstats", [P, CT, 6], CRING)
        work = [[sb(f"fwork{k}_{n}", [P, CT]) for n in range(3)] for k in range(CRING)]
        rstd = sbs("frstd", [P, CT], CRING)
        shift = sbs("fshift", [P, CT], CRING)
        zt = sbs("fzt", [D, L], 2)
        gate_arg = sbs("gate_arg", [P, L], 2)
        gate0 = sbs("gate0_", [P, L], 2)
        proj = sbs("proj", [P, L], 2)
        y_part = sbs("y_part", [P, L], 2)
        y = sbs("y", [P, L], 4)
        y_biased = sbs("y_biased", [P, L], 6)
        yt = sbs("yt", [D, L], 2)
        row_sum = sbs("row_sum", [D, 1], 2)
        right = sbs("right", [D, 1], 2)
        gate1 = sbs("gate1_", [D, L], 2)
        mixed = sbs("mixed", [D, L], 2)
        w_out = sbs("w_out", [D, D], 2)
        normal = sbs("normal", [P, L], 2)
        scaled = sbs("lnscaled", [P, L], 2)
        ps_z, ps_p, ps_q, ps_y, ps_g, ps_l, ps_o = (
            ps(f"ps_{n}") for n in ("z", "p", "q", "y", "g", "l", "o"))

        z_loaded = [sem(f"fz_loaded{k}") for k in range(CRING)]
        x_loaded = [sem(f"fx_loaded{k}") for k in range(CRING)]
        stored = [sem(f"out_stored{k}") for k in range(CRING)]
        z_transposed = sem("z_transposed")
        z_copied = sem("z_copied")
        p_ready = sem("p_ready")
        q_ready = sem("q_ready")
        arg_ready = sem("arg_ready")
        gate0_ready = sem("gate0_ready")
        proj_ready = sem("proj_ready")
        y_part_ready = sem("y_part_ready")
        y_ready = sem("y_ready")
        y_biased_ready = sem("y_biased_ready")
        y_transposed = sem("y_transposed")
        y_copied = sem("y_copied")
        gate1_in_ready = sem("gate1_in_ready")
        left_ready = sem("left_ready")
        gate1_ready = sem("gate1_ready")
        right_ready = sem("right_ready")
        w_out_ready = sem("w_out_ready")
        mixed_ready = sem("mixed_ready")
        out_ready = sem("out_ready")
        summed = sem("summed")
        normal_ready = sem("normal_ready")
        scaled_ready = sem("scaled_ready")
        result_ready = sem("result_ready")
        s_measured = sem("s_measured")
        factor_steps = sem("ffactor_steps")
        chunk_factors = sem("chunk_factors")
        block = ctx.enter_context(nc.Block())
        bodies = L // BODY_R

        def run(engine, step):
            for r in range(BODY_R):
                step(0, r)
            with engine.Fori(1, bodies - 1) as it:
                for r in range(BODY_R):
                    step(it, r)
            for r in range(BODY_R + TO_RESULT):
                step(bodies - 1, r)

        def exists(it, r):
            return not isinstance(it, int) or 0 <= it * BODY_R + r < L

        def chunk_slot(r):
            return (r // CR) % CRING

        def dma_count(it, r):
            return (it + (r // CR) // CRING + 1) * 16

        @block.sync
        def _(sp):
            def load(it, c):
                rows = it * BODY_R + (c - CRING + 1) * CR
                wait(sp, y_ready, rows)
                sp.dma_start(z[c % CRING][:], z_view[it * CRING + c]).then_inc(z_loaded[c % CRING], 16)
                wait(sp, q_ready, rows)
                sp.dma_start(xt[c % CRING][:], x_dram[:, bass.ds((it * CRING + c) * CR * L, CR * L)])\
                    .then_inc(x_loaded[c % CRING], 16)

            def store(it, c):
                sp.wait_ge(result_ready, it * BODY_R + (c + 1) * CR)
                sp.dma_start(out_view[it * CRING + c], result[c % CRING][:])\
                    .then_inc(stored[c % CRING], 16)

            def body(it, first, last):
                for c in range(CRING):
                    if not last:
                        load(it, c + CRING)
                    if not (first and c < 2):
                        store(it, c - 2)

            for c in range(CRING):
                load(0, c)
            body(0, True, False)
            with sp.Fori(1, bodies - 1) as it:
                body(it, False, False)
            body(bodies - 1, False, True)
            store(bodies - 1, CRING - 2)
            store(bodies - 1, CRING - 1)
            for k in range(CRING):
                sp.wait_ge(stored[k], 16 * bodies)

        @block.tensor
        def _(pe):
            ident = const["identity"]

            def transpose_y(it, r):
                n = it * BODY_R + r
                pe.wait_ge(y_ready, n + 1)
                wait(pe, y_copied, n)
                for t in range(LB):
                    last = pe.transpose(ps_y[:, t * P:(t + 1) * P], y[r % 4][:, t * D:(t + 1) * D], ident[:])
                last.then_inc(y_transposed, 1)

            def transpose_z(it, r):
                n = it * BODY_R + r
                if r % CR == 0:
                    pe.wait_ge(z_loaded[chunk_slot(r)], dma_count(it, r))
                wait(pe, z_copied, n)
                for t in range(LB):
                    last = pe.transpose(ps_z[:, t * P:(t + 1) * P],
                                        z[chunk_slot(r)][:, (r % CR) * LB + t], ident[:])
                last.then_inc(z_transposed, 1)

            def project_z(it, r):
                n = it * BODY_R + r
                pe.wait_ge(z_copied, n + 1)
                wait(pe, arg_ready, n)
                for t in range(LB):
                    last = pe.matmul(ps_p[:, t * D:(t + 1) * D], zt[r % 2][:, t * P:(t + 1) * P],
                                     const["Wgo"][:], start=True, stop=True)
                last.then_inc(p_ready, 1)

            def project_x(it, r):
                n = it * BODY_R + r
                if r % CR == 0:
                    pe.wait_ge(x_loaded[chunk_slot(r)], dma_count(it, r))
                wait(pe, proj_ready, n)
                for t in range(LB):
                    at = (r % CR) * L + t * P
                    last = pe.matmul(ps_q[:, t * D:(t + 1) * D], xt[chunk_slot(r)][:, at:at + P],
                                     const["Wo"][:], start=True, stop=True)
                last.then_inc(q_ready, 1)

            def multiply_y(it, r):
                n = it * BODY_R + r
                pe.wait_ge(y_copied, n + 1)
                wait(pe, gate1_ready, n)
                pe.matmul(ps_g[:, 0:L], const["Wg"][:], yt[r % 2][:], start=True, stop=True)\
                    .then_inc(gate1_in_ready, 1)
                wait(pe, mixed_ready, n)
                wait(pe, right_ready, n)
                pe.matmul(ps_l[:, L:L + 1], const["Wr"][:], row_sum[r % 2][:], start=True, stop=True)
                pe.matmul(ps_l[:, 0:L], const["Wle"][:], yt[r % 2][:], start=True, stop=True)\
                    .then_inc(left_ready, 1)

            def multiply_out(it, r):
                n = it * BODY_R + r
                pe.wait_ge(mixed_ready, n + 1)
                pe.wait_ge(w_out_ready, n + 1)
                wait(pe, summed, n)
                for t in range(LB):
                    last = pe.matmul(ps_o[:, t * D:(t + 1) * D], mixed[r % 2][:, t * P:(t + 1) * P],
                                     w_out[r % 2][:], start=True, stop=True)
                last.then_inc(out_ready, 1)

            def step(it, r):
                for part, row in ((transpose_y, r - 1), (transpose_z, r + 2), (project_z, r + 1),
                                  (project_x, r + 1), (multiply_y, r - 1), (multiply_out, r - 3)):
                    if exists(it, row):
                        part(it, row)

            transpose_z(0, 0)
            transpose_z(0, 1)
            project_z(0, 0)
            project_x(0, 0)
            run(pe, step)

        @block.scalar
        def _(act):
            def copy_y(it, r):
                n = it * BODY_R + r
                act.wait_ge(y_transposed, n + 1)
                wait(act, left_ready, n - 1)
                act.activation(yt[r % 2][:], ps_y[:, 0:L], ACT.Identity, accum_out=row_sum[r % 2][:])\
                    .then_inc(y_copied, 1)

            def copy_z(it, r):
                n = it * BODY_R + r
                act.wait_ge(z_transposed, n + 1)
                wait(act, p_ready, n - 1)
                act.activation(zt[r % 2][:], ps_z[:, 0:L], ACT.Identity).then_inc(z_copied, 1)

            def sigmoid0(it, r):
                n = it * BODY_R + r
                act.wait_ge(arg_ready, n + 1)
                wait(act, y_part_ready, n - 1)
                act.activation(gate0[r % 2][:], gate_arg[r % 2][:], ACT.Sigmoid).then_inc(gate0_ready, 1)

            def sigmoid1(it, r):
                n = it * BODY_R + r
                act.wait_ge(gate1_in_ready, n + 1)
                wait(act, mixed_ready, n - 1)
                act.activation(gate1[r % 2][:], ps_g[:, 0:L], ACT.Sigmoid, bias=const["bg"][:, 0:1])\
                    .then_inc(gate1_ready, 1)

            def scale_w_out(it, r):
                n = it * BODY_R + r
                act.wait_ge(right_ready, n + 1)
                wait(act, out_ready, n - 1)
                act.activation(w_out[r % 2][:], const["Wout"][:], ACT.Identity, scale=right[r % 2][:, 0:1])\
                    .then_inc(w_out_ready, 1)

            def normalise(it, r):
                n = it * BODY_R + r
                k = chunk_slot(r)
                if r % CR == 0:
                    act.wait_ge(factor_steps, (it * CRING + r // CR + 1) * factor_ops)
                wait(act, scaled_ready, n - 1)
                for t in range(LB):
                    m = (r % CR) * LB + t
                    last = act.activation(normal[r % 2][:, t * D:(t + 1) * D], s_sum[k][:, m], ACT.Identity,
                                          bias=shift[k][:, m:m + 1], scale=rstd[k][:, m:m + 1])
                last.then_inc(normal_ready, 1)

            def step(it, r):
                for part, row in ((copy_y, r - 1), (copy_z, r + 2), (scale_w_out, r - 3),
                                  (normalise, r - TO_NORM), (sigmoid0, r + 1), (sigmoid1, r - 1)):
                    if exists(it, row):
                        part(it, row)

            copy_z(0, 0)
            copy_z(0, 1)
            sigmoid0(0, 0)
            run(act, step)

        @block.vector
        def _(dve):
            def fetch_factors(it, c):
                dve.tensor_copy(rstd_zx[c % CRING][:], const["rstd"][:, :, bass.ds((it * CRING + c) * CT, CT)])\
                    .then_inc(chunk_factors, 1)

            def chunk_moments(it, c):
                dve.wait_ge(s_measured, it * BODY_R + (c + 1) * CR)
                wait(dve, normal_ready, it * BODY_R + (c + 1 - CRING) * CR)
                k = c % CRING
                moments(dve, stats[k][:], [x[:] for x in work[k]], factor_steps,
                        (it * CRING + c) * factor_ops)

            def refine(it, c, n):
                k = c % CRING
                double_mean, variance, term = work[k]
                root = rstd[k]
                dve.wait_ge(factor_steps, (it * CRING + c) * factor_ops + MOMENT_STEPS + n)
                if n == 0:
                    done = dve.tensor_scalar(variance[:], variance[:], 1.0 / D, EPS, ALU.mult, ALU.add)
                elif n == 1:
                    done = dve.tensor_scalar(root[:].bitcast(I32), variance[:].bitcast(I32), -0.5, RSQRT_BITS,
                                             ALU.mult, ALU.add)
                elif n == refine_steps - 1:
                    done = dve.scalar_tensor_tensor(shift[k][:], double_mean[:], -0.5, root[:],
                                                    ALU.mult, ALU.mult)
                elif (n - 2) % 3 == 0:
                    done = dve.tensor_tensor(term[:], root[:], root[:], ALU.mult)
                elif (n - 2) % 3 == 1:
                    done = dve.scalar_tensor_tensor(term[:], term[:], -0.5, variance[:], ALU.mult, ALU.mult)
                else:
                    done = dve.scalar_tensor_tensor(root[:], term[:], 1.5, root[:], ALU.add, ALU.mult)
                done.then_inc(factor_steps, 1)

            def add_bias(it, r, bank, factor, bias, to, done):
                for t in range(LB):
                    m = (r % CR) * LB + t
                    last = dve.scalar_tensor_tensor(
                        to[r % 2][:, t * D:(t + 1) * D], bank[:, t * D:(t + 1) * D],
                        factor[:, m:m + 1], bias[:], ALU.mult, ALU.add)
                last.then_inc(done, 1)

            def gate_argument(it, r):
                n = it * BODY_R + r
                if r % CR == 0:
                    dve.wait_ge(chunk_factors, it * CRING + r // CR + 1)
                dve.wait_ge(p_ready, n + 1)
                wait(dve, gate0_ready, n - 1)
                add_bias(it, r, ps_p, rstd_zx[chunk_slot(r)][:, 0], const["bgo"], gate_arg, arg_ready)

            def projection(it, r):
                n = it * BODY_R + r
                dve.wait_ge(q_ready, n + 1)
                wait(dve, y_part_ready, n - 1)
                add_bias(it, r, ps_q, rstd_zx[chunk_slot(r)][:, 1], const["bo"], proj, proj_ready)

            def mix(it, r):
                n = it * BODY_R + r
                dve.wait_ge(left_ready, n + 1)
                wait(dve, w_out_ready, n - 1)
                dve.tensor_tensor(right[r % 2][:], ps_l[:, L:L + 1], const["br"][:], ALU.add)\
                    .then_inc(right_ready, 1)
                dve.wait_ge(gate1_ready, n + 1)
                wait(dve, out_ready, n - 1)
                dve.scalar_tensor_tensor(mixed[r % 2][:], ps_l[:, 0:L], const["ble"][:, 0:1],
                                         gate1[r % 2][:], ALU.add, ALU.mult).then_inc(mixed_ready, 1)

            def add_residual(it, r):
                n = it * BODY_R + r
                k = chunk_slot(r)
                dve.wait_ge(out_ready, n + 1)
                dve.wait_ge(y_biased_ready, n + 1)
                if r % CR == 0:
                    wait(dve, normal_ready, n - (CRING - 1) * CR)
                m = (r % CR) * LB
                dve.tensor_tensor(s_sum[k][:, m:m + LB].rearrange("p t c -> p (t c)"), ps_o[:, 0:L],
                                  y_biased[r % 6][:], ALU.add).then_inc(summed, 1)

            def measure_s(it, r):
                n = it * BODY_R + r
                k = chunk_slot(r)
                dve.wait_ge(summed, n + 1)
                for t in range(LB):
                    m = (r % CR) * LB + t
                    last = dve.bn_stats(stats[k][:, m], s_sum[k][:, m])
                last.then_inc(s_measured, 1)

            def scale_result(it, r):
                n = it * BODY_R + r
                dve.wait_ge(normal_ready, n + 1)
                wait(dve, result_ready, n - 1)
                dve.tensor_tensor(scaled[r % 2][:], normal[r % 2][:], const["ln_scale"][:],
                                  ALU.mult).then_inc(scaled_ready, 1)

            def step(it, r):
                parts = ((add_residual, r - TO_SUM), (mix, r - 2), (scale_result, r - TO_RESULT),
                         (measure_s, r - TO_SUM), (gate_argument, r + 1), (projection, r + 1))
                c = (r - TO_SUM - CR + 1) // CR
                since = (r - TO_SUM - CR + 1) % CR * len(parts)
                for p, (part, row) in enumerate(parts):
                    if exists(it, row):
                        part(it, row)
                    if exists(it, c * CR):
                        if since + p == 3:
                            chunk_moments(it, c)
                        if 0 <= since + p - 4 < refine_steps:
                            refine(it, c, since + p - 4)
                if r % CR == 1 and exists(it, r + 3):
                    fetch_factors(it, (r + 3) // CR)

            fetch_factors(0, 0)
            gate_argument(0, 0)
            projection(0, 0)
            run(dve, step)

        @block.gpsimd
        def _(pool):
            def residual0(it, r):
                n = it * BODY_R + r
                pool.wait_ge(proj_ready, n + 1)
                pool.wait_ge(gate0_ready, n + 1)
                pool.tensor_tensor(y_part[r % 2][:], proj[r % 2][:], gate0[r % 2][:],
                                          ALU.mult).then_inc(y_part_ready, 1)
                wait(pool, y_transposed, n - 1)
                pool.wait_ge(y_part_ready, n + 1)
                m = (r % CR) * LB
                pool.tensor_tensor(y[r % 4][:], y_part[r % 2][:],
                                   z[chunk_slot(r)][:, m:m + LB].rearrange("p t c -> p (t c)"),
                                   ALU.add).then_inc(y_ready, 1)

            def add_out_bias(it, r):
                n = it * BODY_R + r
                pool.wait_ge(y_ready, n + 1)
                wait(pool, summed, n - 5)
                pool.tensor_tensor(y_biased[r % 6][:], y[r % 4][:], const["bout"][:],
                                          ALU.add).then_inc(y_biased_ready, 1)

            def shift_result(it, r):
                n = it * BODY_R + r
                k = chunk_slot(r)
                if r % CR == 0:
                    wait(pool, stored[k], dma_count(it, r) - 16)
                pool.wait_ge(scaled_ready, n + 1)
                m = (r % CR) * LB
                pool.tensor_tensor(result[k][:, m:m + LB].rearrange("p t c -> p (t c)"),
                                          scaled[r % 2][:], const["ln_bias"][:],
                                          ALU.add).then_inc(result_ready, 1)

            def step(it, r):
                for part, row in ((residual0, r + 1), (shift_result, r - TO_RESULT), (add_out_bias, r + 1)):
                    if exists(it, row):
                        part(it, row)

            residual0(0, 0)
            add_out_bias(0, 0)
            run(pool, step)


_WEIGHTS = {"Wa": ("L0_conv_Wa", True), "Wga": ("L0_conv_Wga", True), "Wb": ("L0_conv_Wb", True),
            "Wgb": ("L0_conv_Wgb", True), "Wo": ("L0_conv_Wo", True), "Wgo": ("L0_conv_Wgo", True),
            "Wl": ("L1_conv_W_left", False), "We": ("L1_conv_W_eq", False),
            "Wr": ("L1_conv_W_right", False), "Wg": ("L1_conv_W_gate", False),
            "Wout": ("L1_conv_W_out", False)}
_VECTORS = {"norm_g": "L0_conv_norm_g", "norm_b": "L0_conv_norm_b", "normo_g": "L0_conv_normo_g",
            "normo_b": "L0_conv_normo_b", "ba": "L0_conv_ba", "bga": "L0_conv_bga", "bb": "L0_conv_bb",
            "bgb": "L0_conv_bgb", "bo": "L0_conv_bo", "bgo": "L0_conv_bgo", "bl": "L1_conv_b_left",
            "be": "L1_conv_b_eq", "br": "L1_conv_b_right", "bg": "L1_conv_b_gate",
            "bout": "L1_conv_b_out", "ln_scale": "L1_conv_ln_scale", "ln_bias": "L1_conv_ln_bias"}


def kernel(**inputs):
    import concourse.bacc as bacc
    import numpy as np
    from concourse.bass_utils import run_bass_kernel_spmd

    nc = bacc.Bacc("TRN2", target_bir_lowering=False, num_devices=1)
    arrays = {}

    def give(name, array):
        array = np.ascontiguousarray(array)
        arrays[name] = array
        return nc.dram_tensor(name, array.shape, mybir.dt.from_np(array.dtype), kind="ExternalInput").ap()

    x = give("x_in", np.asarray(inputs["x"]))
    w = {n: give("w_" + n, np.asarray(inputs[k]).T if turned else np.asarray(inputs[k]))
         for n, (k, turned) in _WEIGHTS.items()}
    vec = {n: give("v_" + n, np.asarray(inputs[k])) for n, k in _VECTORS.items()}
    out = nc.dram_tensor("out", (1, L, L, D), F32, kind="ExternalOutput").ap()
    bass_pair_layers(nc, x, w, vec, out)
    r = run_bass_kernel_spmd(nc, [arrays], core_ids=[0])
    return r.results[0]["out"]
```

```python
from contextlib import ExitStack

import concourse.bass as bass
from concourse import mybir

F32 = mybir.dt.float32
F32R = mybir.dt.float32r
I32 = mybir.dt.int32
ALU = mybir.AluOpType
ACT = mybir.ActivationFunctionType

P = 128
D = 128
L = 384
LB = L // P
TOKENS = L * L
PITCH = TOKENS + 1024
EPS = 1e-5

GT = 4
GROUP = GT * P
GROUPS = TOKENS // GROUP
LOAD_G = 2
LOAD_RING = 6
BATCH_G = 4
BODY_G = 12
BATCH_RING = BODY_G // BATCH_G
STATS_AHEAD = 8
NORM_POOL = 3

CR = 4
CT = CR * LB
CRING = 3
BODY_R = CR * CRING
FR = 6
FT = FR * LB
FRING = BODY_R // FR
TO_SUM = 4
TO_NORM = 12
TO_RESULT = 13


def wait(engine, semaphore, value):
    if isinstance(value, int) and value <= 0:
        return
    engine.wait_ge(semaphore, value)


MOMENT_STEPS = 5

RSQRT_BITS = float(0x5F3759DF)
NEWTON_STEPS = 3


def moments(dve, stats, work, steps, base):
    double_mean, total, square = work
    dve.tensor_tensor(double_mean, stats[..., 1], stats[..., 4], ALU.subtract).then_inc(steps, 1)
    dve.tensor_tensor(total, stats[..., 2], stats[..., 5], ALU.add).then_inc(steps, 1)
    dve.wait_ge(steps, base + 1)
    dve.scalar_tensor_tensor(square, double_mean, D / 4.0, double_mean, ALU.mult, ALU.mult)\
        .then_inc(steps, 1)
    dve.wait_ge(steps, base + 3)
    dve.tensor_tensor(total, total, square, ALU.add).then_inc(steps, 1)
    dve.tensor_tensor(double_mean, stats[..., 1], stats[..., 4], ALU.add).then_inc(steps, 1)


def bass_pair_layers(nc, x, weights, columns, rows, out):
    a_dram = nc.dram_tensor("a_scratch", (D, PITCH), F32, kind="Internal").ap()[:, 0:TOKENS]
    b_dram = nc.dram_tensor("b_scratch", (D, PITCH), F32, kind="Internal").ap()[:, 0:TOKENS]
    x_dram = nc.dram_tensor("x_scratch", (D, PITCH), F32, kind="Internal").ap()[:, 0:TOKENS]
    z_flat = x.rearrange("b i j c -> (b i j) c")
    out_flat = out.rearrange("b i j c -> (b i j) c")

    with ExitStack() as ctx:
        def sb(name, shape, dt=F32):
            return ctx.enter_context(nc.sbuf_tensor(name, shape, dt))

        const = {
            "identity": sb("identity", [P, P]),
            "rstd": sb("rstd_zx", [P, 2, TOKENS // P]),
        }
        for n in ("Wa", "Wga", "Wb", "Wgb"):
            const[n + "_high"] = sb(n + "_high", [D, D], F32R)
            const[n + "_low"] = sb(n + "_low", [D, D], F32R)
        for n in ("Wgo", "Wo", "Wle"):
            const[n] = sb(n + "_c", [D, D])
        for n in ("ba", "bga", "bb", "bgb", "ble", "br"):
            const[n] = sb(n + "_col", [D, 1])
        for n in ("bgo", "bo"):
            const[n] = sb(n + "_row", [P, D])
        raw = {"weights": sb("raw_weights", [D, len(WEIGHTS), D]), "columns": sb("raw_columns", [D, len(COLUMNS)]),
               "rows": sb("raw_rows", [P, ROWS_SIZE])}
        raw.update((n, raw["weights"][:, k]) for k, n in enumerate(WEIGHTS))
        for n in ("Wg", "Wr", "Wout"):
            const[n] = raw[n]
        const["bg"] = raw["columns"][:, COLUMNS.index("bg"):COLUMNS.index("bg") + 1]
        at = 0
        for n, copies in ROWS:
            raw[n + "_row"] = raw["rows"][:, at:at + copies * D]
            at += copies * D
        for n in ("bout", "ln_scale", "ln_bias"):
            const[n] = raw[n + "_row"]

        prepare(nc, weights, columns, rows, raw, const)
        project(nc, z_flat, a_dram, b_dram, const)
        triangle(nc, a_dram, b_dram, x_dram, const)
        finish(nc, z_flat, x_dram, out_flat, const)


WEIGHTS = ("Wa", "Wga", "Wb", "Wgb", "Wgo", "Wo", "Wl", "We", "Wg", "Wr", "Wout")
COLUMNS = ("norm_g", "norm_b", "normo_g", "normo_b", "ba", "bga", "bb", "bgb", "bl", "be", "br", "bg")
ROWS = (("bgo", 1), ("bo", 1), ("bout", LB), ("ln_scale", LB), ("ln_bias", LB))
ROWS_SIZE = sum(copies for _, copies in ROWS) * D


def prepare(nc, weights, columns, rows, raw, const):
    with ExitStack() as ctx:
        def sb(name, shape, dt=F32):
            return ctx.enter_context(nc.sbuf_tensor(name, shape, dt))

        def sem(name):
            return ctx.enter_context(nc.semaphore(name))

        gated = ("Wa", "Wga", "Wb", "Wgb")
        scaled = {n: sb("scaled_" + n, [D, D]) for n in (*gated, "Wgo", "Wo")}
        col = {n: raw["columns"][:, k:k + 1] for k, n in enumerate(COLUMNS)}
        row = {n: raw[n + "_row"] for n in ("bgo", "bo")}
        spread = {n: sb("spread_" + n, [D, P]) for n in ("norm_b", "normo_b")}
        ones = sb("ones", [D, P])
        inv_d = sb("inv_d", [D, P])
        psum_col = ctx.enter_context(nc.psum_tensor("prep_col", [D, 4], F32))
        psum_row = [ctx.enter_context(nc.psum_tensor(f"prep_row{k}", [P, D], F32)) for k in range(2)]
        psum_mean = [ctx.enter_context(nc.psum_tensor(f"prep_mean{k}", [P, D], F32)) for k in range(2)]

        loaded = sem("prep_loaded")
        filled = sem("prep_filled")
        chain = sem("prep_chain")
        multiplied = sem("prep_multiplied")
        block = ctx.enter_context(nc.Block())

        loads = ((raw["columns"][:], columns), (raw["weights"][:], weights),
                 (raw["rows"][:], rows.partition_broadcast(P)))

        @block.sync
        def _(sp):
            for to, of in loads:
                sp.dma_start(to, of).then_inc(loaded, 16)

        @block.gpsimd
        def _(pool):
            pool.memset(const["identity"][:], 0.0).then_inc(filled, 1)
            pool.wait_ge(filled, 1)
            pool.affine_select(out=const["identity"][:], in_=const["identity"][:],
                               compare_op=ALU.not_equal, fill=1.0, base=0,
                               pattern=[[-1, P]], channel_multiplier=1).then_inc(filled, 1)

        @block.vector
        def _(dve):
            count = [0]

            def step(ins):
                ins.then_inc(chain, 1)
                count[0] += 1

            def settle():
                dve.wait_ge(chain, count[0])

            step(dve.memset(ones[:], 1.0))
            step(dve.memset(inv_d[:], 1.0 / D))
            settle()
            dve.wait_ge(loaded, 16 * len(loads))
            for n, v in (("norm_b", "norm_b"), ("normo_b", "normo_b")):
                step(dve.tensor_scalar(spread[n][:], ones[:], col[v][:, 0:1], None, ALU.mult))
            for n in (*gated, "Wgo"):
                step(dve.tensor_scalar(scaled[n][:], raw[n][:], col["norm_g"][:, 0:1], None, ALU.mult))
            step(dve.tensor_scalar(scaled["Wo"][:], raw["Wo"][:], col["normo_g"][:, 0:1], None, ALU.mult))
            step(dve.tensor_tensor(const["Wle"][:], raw["Wl"][:], raw["We"][:], ALU.add))
            step(dve.tensor_tensor(const["ble"][:], col["bl"][:], col["be"][:], ALU.add))
            step(dve.tensor_scalar(const["br"][:], col["br"][:], float(L), None, ALU.mult))
            settle()
            assert count[0] == SCALED
            for n in gated:
                step(dve.tensor_copy(const[n + "_high"][:], scaled[n][:]))
            settle()
            for n in gated:
                step(dve.tensor_tensor(const[n + "_low"][:], scaled[n][:],
                                       const[n + "_high"][:].bitcast(F32), ALU.subtract))
            dve.wait_ge(multiplied, 8)
            for k, n in enumerate(("ba", "bga", "bb", "bgb")):
                step(dve.tensor_tensor(const[n][:], psum_col[:, k:k + 1], col[n][:], ALU.add))
            for k, n in enumerate(("bgo", "bo")):
                step(dve.tensor_tensor(const[n][:], psum_row[k][:], row[n][:], ALU.add))
            for k, n in enumerate(("Wgo", "Wo")):
                step(dve.tensor_tensor(const[n][:], scaled[n][:], psum_mean[k][:], ALU.subtract))
            settle()

        @block.tensor
        def _(pe):
            pe.wait_ge(loaded, 16 * len(loads))
            pe.wait_ge(chain, SCALED)
            for k, n in enumerate(gated):
                pe.matmul(psum_col[:, k:k + 1], raw[n][:], col["norm_b"][:], start=True, stop=True)\
                    .then_inc(multiplied, 1)
            for k, (n, v) in enumerate((("Wgo", "norm_b"), ("Wo", "normo_b"))):
                pe.matmul(psum_row[k][:], spread[v][:], raw[n][:], start=True, stop=True)\
                    .then_inc(multiplied, 1)
                pe.matmul(psum_mean[k][:], inv_d[:], scaled[n][:], start=True, stop=True)\
                    .then_inc(multiplied, 1)


SCALED = 2 + 2 + 5 + 1 + 3


def project(nc, z_flat, a_dram, b_dram, const):
    z_view = z_flat.rearrange("(n t p) c -> n p t c", p=P, t=LOAD_G * GT)
    batch = BATCH_G * GROUP
    tiles = BATCH_G * GT
    stats_ops = tiles + MOMENT_STEPS + 2
    factor_ops = 3

    with ExitStack() as ctx:
        def sb(name, shape, dt=F32):
            return ctx.enter_context(nc.sbuf_tensor(name, shape, dt))

        def ps(name):
            return ctx.enter_context(nc.psum_tensor(name, [P, GROUP], F32))

        def sem(name):
            return ctx.enter_context(nc.semaphore(name))

        z = [sb(f"z{k}", [P, LOAD_G * GT, D]) for k in range(LOAD_RING)]
        stats = [sb(f"stats{k}", [P, tiles, 6]) for k in range(BATCH_RING)]
        work = [[sb(f"stats_work{k}_{n}", [P, tiles]) for n in range(3)] for k in range(BATCH_RING)]
        power = sb("power", [P, tiles])
        rstd = [sb(f"rstd{k}", [P, tiles]) for k in range(BATCH_RING)]
        shift = [sb(f"shift{k}", [P, tiles]) for k in range(BATCH_RING)]
        zn = [sb(f"zn{k}", [P, GROUP]) for k in range(4)]
        zt_high = [sb(f"zt_high{k}", [D, GROUP], F32R) for k in range(2)]
        zt_low = [sb(f"zt_low{k}", [D, GROUP], F32R) for k in range(2)]
        gate = [sb(f"gate{k}", [D, GROUP]) for k in range(2)]
        gated_out = [[sb(f"gated{h}_{k}", [D, batch]) for k in range(BATCH_RING)] for h in range(2)]
        ps_zt = [ps(f"ps_zt{k}") for k in range(2)]
        ps_gate = [ps(f"ps_gate{k}") for k in range(2)]
        ps_lin = [ps(f"ps_lin{k}") for k in range(4)]

        z_loaded = [sem(f"z_loaded{k}") for k in range(LOAD_RING)]
        stats_steps = sem("stats_steps")
        factor_steps = sem("factor_steps")
        power_filled = sem("power_filled")
        normed = sem("normed")
        normed_pool = sem("normed_pool")
        scaled_pool = sem("scaled_pool")
        transposed = sem("transposed")
        high_done = sem("high_done")
        low_done = sem("low_done")
        multiplied = sem("multiplied")
        sigmoid_done = sem("sigmoid_done")
        gated = sem("gated")
        stored = [[sem(f"stored{h}_{k}") for k in range(BATCH_RING)] for h in range(2)]
        block = ctx.enter_context(nc.Block())

        weights = [("Wga", "Wa"), ("Wgb", "Wb")]
        biases = [("bga", "ba"), ("bgb", "bb")]
        loads_per_body = BODY_G // LOAD_G
        batches_per_body = BODY_G // BATCH_G
        bodies = GROUPS // BODY_G

        def run(engine, body):
            body(0, True, False)
            with engine.Fori(1, bodies - 1) as it:
                body(it, False, False)
            body(bodies - 1, False, True)

        def exists(g, last):
            return not last or g < BODY_G

        @block.sync
        def _(sp):
            def load(it, k):
                wait(sp, normed, it * BODY_G + LOAD_G * (k - LOAD_RING + 1))
                wait(sp, normed_pool, it * BODY_G + LOAD_G * (k - LOAD_RING + 1))
                sp.dma_start(z[k % LOAD_RING][:], z_view[it * loads_per_body + k])\
                    .then_inc(z_loaded[k % LOAD_RING], 16)

            def body(it, first, last):
                for j in range(batches_per_body):
                    for k in range(2 * j, 2 * j + 2):
                        if not last:
                            load(it, k + LOAD_RING)
                    for h, to in enumerate((a_dram, b_dram)):
                        sp.wait_ge(gated, it * 2 * BODY_G + 2 * BATCH_G * (j + 1) - 1 + h)
                        sp.dma_start(to[:, bass.ds((it * batches_per_body + j) * batch, batch)],
                                     gated_out[h][j][:]).then_inc(stored[h][j], 16)

            for k in range(LOAD_RING):
                load(0, k)
            run(sp, body)
            for h in range(2):
                for k in range(BATCH_RING):
                    sp.wait_ge(stored[h][k], 16 * bodies)

        @block.vector
        def _(dve):
            def measure(it, g):
                k = g // LOAD_G
                if g % LOAD_G == 0:
                    dve.wait_ge(z_loaded[k % LOAD_RING], (it + k // LOAD_RING + 1) * 16)
                for t in range(GT):
                    dve.bn_stats(stats[(g // BATCH_G) % BATCH_RING][:, (g % BATCH_G) * GT + t, :],
                                 z[k % LOAD_RING][:, (g % LOAD_G) * GT + t, :]).then_inc(stats_steps, 1)

            def close(it, b):
                k = b % BATCH_RING
                base = (it * batches_per_body + b) * stats_ops + tiles
                dve.wait_ge(stats_steps, base)
                wait(dve, factor_steps, (it * batches_per_body + b - BATCH_RING + 1) * factor_ops)
                moments(dve, stats[k][:], [x[:] for x in work[k]], stats_steps, base)
                dve.wait_ge(stats_steps, base + MOMENT_STEPS)
                dve.tensor_scalar(work[k][1][:], work[k][1][:], 1.0 / D, EPS, ALU.mult, ALU.add)\
                    .then_inc(stats_steps, 1)
                dve.tensor_scalar(work[k][0][:], work[k][0][:], -0.5, None, ALU.mult)\
                    .then_inc(stats_steps, 1)

            def low(it, g):
                dve.wait_ge(high_done, it * BODY_G + g + 1)
                dve.tensor_tensor(zt_low[g % 2][:], ps_zt[g % 2][:], zt_high[g % 2][:].bitcast(F32),
                                  ALU.subtract).then_inc(low_done, 1)

            def apply_gate(it, g, h):
                u = 2 * g + h
                if g % BATCH_G == 0:
                    wait(dve, stored[h][g // BATCH_G], 16 * it)
                dve.wait_ge(sigmoid_done, it * 2 * BODY_G + u + 1)
                dve.wait_ge(multiplied, it * 4 * BODY_G + 2 * u + 2)
                at = (g % BATCH_G) * GROUP
                dve.scalar_tensor_tensor(gated_out[h][g // BATCH_G][:, at:at + GROUP],
                                         ps_lin[u % 4][:], const[biases[h][1]][:, 0:1],
                                         gate[u % 2][:], ALU.add, ALU.mult).then_inc(gated, 1)

            def body(it, first, last):
                for g in range(BODY_G):
                    if exists(g + 1, last):
                        low(it, g + 1)
                    if exists(g + STATS_AHEAD, last):
                        measure(it, g + STATS_AHEAD)
                        if (g + STATS_AHEAD) % BATCH_G == BATCH_G - 1:
                            close(it, (g + STATS_AHEAD) // BATCH_G)
                    for h in range(2):
                        apply_gate(it, g, h)

            for g in range(STATS_AHEAD):
                measure(0, g)
                if g % BATCH_G == BATCH_G - 1:
                    close(0, g // BATCH_G)
            low(0, 0)
            run(dve, body)

        @block.scalar
        def _(act):
            def normalise(it, g):
                b = g // BATCH_G
                if g % BATCH_G == 0:
                    act.wait_ge(factor_steps, (it * batches_per_body + b) * factor_ops + 2)
                wait(act, transposed, it * BODY_G + g - 3)
                tiles_here = [t for t in range(GT) if t != NORM_POOL]
                for t in tiles_here:
                    n = (g % BATCH_G) * GT + t
                    last = act.activation(zn[g % 4][:, t * D:(t + 1) * D],
                                          z[(g // LOAD_G) % LOAD_RING][:, (g % LOAD_G) * GT + t, :],
                                          ACT.Identity, bias=shift[b % BATCH_RING][:, n:n + 1],
                                          scale=rstd[b % BATCH_RING][:, n:n + 1])
                last.then_inc(normed, 1)

            def high(it, g):
                act.wait_ge(transposed, it * BODY_G + g + 1)
                wait(act, multiplied, it * 4 * BODY_G + 4 * (g - 1))
                act.activation(zt_high[g % 2][:], ps_zt[g % 2][:], ACT.Identity).then_inc(high_done, 1)

            def sigmoid(it, g, h):
                u = 2 * g + h
                act.wait_ge(multiplied, it * 4 * BODY_G + 2 * u + 1)
                wait(act, gated, it * 2 * BODY_G + u - 1)
                act.activation(gate[u % 2][:], ps_gate[u % 2][:], ACT.Sigmoid,
                               bias=const[biases[h][0]][:, 0:1]).then_inc(sigmoid_done, 1)

            def body(it, first, last):
                for g in range(BODY_G):
                    if exists(g + 1, last):
                        high(it, g + 1)
                    if exists(g + 2, last):
                        normalise(it, g + 2)
                    for h in range(2):
                        sigmoid(it, g, h)

            normalise(0, 0)
            normalise(0, 1)
            high(0, 0)
            run(act, body)

        @block.gpsimd
        def _(pool):
            def factors(it, b):
                k = b % BATCH_RING
                n = it * batches_per_body + b
                pool.wait_ge(stats_steps, (n + 1) * stats_ops)
                wait(pool, normed, it * BODY_G + BATCH_G * (b - BATCH_RING + 1))
                wait(pool, normed_pool, it * BODY_G + BATCH_G * (b - BATCH_RING + 1))
                pool.tensor_tensor(rstd[k][:], work[k][1][:], power[:], ALU.pow).then_inc(factor_steps, 1)
                pool.wait_ge(factor_steps, n * factor_ops + 1)
                pool.tensor_tensor(shift[k][:], work[k][0][:], rstd[k][:], ALU.mult).then_inc(factor_steps, 1)
                pool.tensor_copy(const["rstd"][:, 0, bass.ds(n * tiles, tiles)], rstd[k][:])\
                    .then_inc(factor_steps, 1)

            def normalise(it, g):
                b = g // BATCH_G
                if g % BATCH_G == 0:
                    pool.wait_ge(factor_steps, (it * batches_per_body + b) * factor_ops + 2)
                wait(pool, transposed, it * BODY_G + g - 3)
                t = NORM_POOL
                n = (g % BATCH_G) * GT + t
                to = zn[g % 4][:, t * D:(t + 1) * D]
                pool.tensor_tensor(to, z[(g // LOAD_G) % LOAD_RING][:, (g % LOAD_G) * GT + t, :],
                                   rstd[b][:, n:n + 1].to_broadcast([P, D]), ALU.mult).then_inc(scaled_pool, 1)
                pool.wait_ge(scaled_pool, it * BODY_G + g + 1)
                pool.tensor_tensor(to, to, shift[b][:, n:n + 1].to_broadcast([P, D]), ALU.add)\
                    .then_inc(normed_pool, 1)

            def body(it, first, last):
                for g in range(BODY_G):
                    if g % BATCH_G == 0:
                        factors(it, g // BATCH_G)
                    normalise(it, g)

            pool.memset(power[:], -0.5).then_inc(power_filled, 1)
            pool.wait_ge(power_filled, 1)
            run(pool, body)

        @block.tensor
        def _(pe):
            def transpose(it, g):
                pe.wait_ge(normed, it * BODY_G + g + 1)
                pe.wait_ge(normed_pool, it * BODY_G + g + 1)
                wait(pe, low_done, it * BODY_G + g - 1)
                for t in range(GT):
                    last = pe.transpose(ps_zt[g % 2][:, t * P:(t + 1) * P], zn[g % 4][:, t * D:(t + 1) * D],
                                        const["identity"][:])
                last.then_inc(transposed, 1)

            def multiply(it, g):
                pe.wait_ge(low_done, it * BODY_G + g + 1)
                for h in range(2):
                    u = 2 * g + h
                    for name, bank, free, count in (
                            (weights[h][0], ps_gate[u % 2], sigmoid_done, u - 1),
                            (weights[h][1], ps_lin[u % 4], gated, u - 3)):
                        wait(pe, free, it * 2 * BODY_G + count)
                        w_high, w_low = const[name + "_high"], const[name + "_low"]
                        pe.matmul(bank[:], w_low[:], zt_high[g % 2][:], start=True, stop=False)
                        pe.matmul(bank[:], w_high[:], zt_low[g % 2][:], start=False, stop=False)
                        pe.matmul(bank[:], w_high[:], zt_high[g % 2][:], start=False, stop=True)\
                            .then_inc(multiplied, 1)

            def body(it, first, last):
                for g in range(BODY_G):
                    if exists(g + 1, last):
                        transpose(it, g + 1)
                    multiply(it, g)

            transpose(0, 0)
            run(pe, body)


def triangle(nc, a_dram, b_dram, x_dram, const):
    a_view = a_dram.rearrange("d (n p j) -> d p n j", p=P, n=LB)
    b_view = b_dram.rearrange("d (n p j) -> d p n j", p=P, n=LB)
    x_view = x_dram.rearrange("d (n p j) -> d p n j", p=P, n=LB)
    ring = 4

    with ExitStack() as ctx:
        def sb(name, shape, dt=F32):
            return ctx.enter_context(nc.sbuf_tensor(name, shape, dt))

        def ps(name):
            return ctx.enter_context(nc.psum_tensor(name, [P, 512], F32))

        def sem(name):
            return ctx.enter_context(nc.semaphore(name))

        a_raw = [sb(f"a_raw{k}", [P, LB, L]) for k in range(ring)]
        b_raw = [sb(f"b_raw{k}", [P, LB, L]) for k in range(ring)]
        at_high = [sb(f"at_high{k}", [P, LB, L], F32R) for k in range(2)]
        at_low = [sb(f"at_low{k}", [P, LB, L], F32R) for k in range(2)]
        b_high = [sb(f"b_high{k}", [P, LB, L], F32R) for k in range(2)]
        b_low = [sb(f"b_low{k}", [P, LB, L], F32R) for k in range(2)]
        x_out = [sb(f"x_out{k}", [P, LB, L]) for k in range(2)]
        x_square = [sb(f"x_square{k}", [P, LB, L]) for k in range(2)]
        x_sum = sb("x_sum", [P, LB, L])
        square_sum = sb("square_sum", [P, LB, L])
        x_var = sb("x_var", [P, LB, L])
        eps = sb("x_eps", [P, 1])
        ps_at = [ps(f"ps_at{k}") for k in range(LB)]
        ps_x = [ps(f"ps_x{k}") for k in range(LB)]

        a_loaded = [sem(f"a_loaded{k}") for k in range(ring)]
        b_loaded = [sem(f"b_loaded{k}") for k in range(ring)]
        a_transposed = sem("a_transposed")
        a_high_done = sem("a_high_done")
        a_low_done = sem("a_low_done")
        x_multiplied = sem("x_multiplied")
        x_copied = sem("x_copied")
        x_squared = sem("x_squared")
        x_summed = sem("x_summed")
        squares_summed = sem("squares_summed")
        sums_cleared = sem("sums_cleared")
        x_factor_steps = sem("x_factor_steps")
        x_std_ready = sem("x_std_ready")
        x_factor_transposed = sem("x_factor_transposed")
        b_high_done = sem("b_high_done")
        b_low_done = sem("b_low_done")
        x_stored = [sem(f"x_stored{k}") for k in range(2)]
        block = ctx.enter_context(nc.Block())
        bodies = D // ring

        def run(engine, body):
            body(0, False)
            with engine.Fori(1, bodies - 1) as it:
                body(it, False)
            body(bodies - 1, True)

        def exists(d, last):
            return not last or d < ring

        @block.sync
        def _(sp):
            def load(it, d):
                wait(sp, a_transposed, (it * ring + d - ring + 1) * LB)
                sp.dma_start(a_raw[d % ring][:], a_view[it * ring + d]).then_inc(a_loaded[d % ring], 16)
                wait(sp, b_low_done, it * ring + d - ring + 1)
                sp.dma_start(b_raw[d % ring][:], b_view[it * ring + d]).then_inc(b_loaded[d % ring], 16)

            def body(it, last):
                for d in range(ring):
                    if exists(d + ring, last):
                        load(it, d + ring)
                    sp.wait_ge(x_copied, (it * ring + d + 1) * LB)
                    sp.dma_start(x_view[it * ring + d], x_out[d % 2][:]).then_inc(x_stored[d % 2], 16)

            for d in range(ring):
                load(0, d)
            run(sp, body)
            for k in range(2):
                sp.wait_ge(x_stored[k], 16 * D // 2)

        @block.vector
        def _(dve):
            def split(it, d):
                n = it * ring + d
                dve.wait_ge(b_loaded[d % ring], (it + d // ring + 1) * 16)
                wait(dve, x_multiplied, (n - 1) * LB)
                dve.tensor_copy(b_high[d % 2][:], b_raw[d % ring][:]).then_inc(b_high_done, 1)
                for j in range(LB):
                    dve.wait_ge(a_high_done, n * LB + j + 1)
                    dve.tensor_tensor(at_low[d % 2][:, j], ps_at[j][:, 0:L],
                                      at_high[d % 2][:, j].bitcast(F32), ALU.subtract)\
                        .then_inc(a_low_done, 1)
                dve.wait_ge(b_high_done, n + 1)
                dve.tensor_tensor(b_low[d % 2][:], b_raw[d % ring][:], b_high[d % 2][:].bitcast(F32),
                                  ALU.subtract).then_inc(b_low_done, 1)

            def add(it, d):
                n = it * ring + d
                for i in range(LB):
                    dve.wait_ge(x_squared, n * LB + i + 1)
                    wait(dve, x_summed, (n - 1) * LB + i + 1)
                    dve.tensor_tensor(x_sum[:, i], ps_x[i][:, 0:L], x_sum[:, i], ALU.add).then_inc(x_summed, 1)

            def body(it, last):
                for d in range(ring):
                    if exists(d + 1, last):
                        split(it, d + 1)
                    add(it, d)

            def x_factors():
                dve.wait_ge(x_summed, D * LB)
                dve.wait_ge(squares_summed, D)
                for i in range(LB):
                    dve.scalar_tensor_tensor(x_var[:, i], x_sum[:, i], -1.0 / D, x_sum[:, i],
                                             ALU.mult, ALU.mult).then_inc(x_factor_steps, 1)
                for i in range(LB):
                    dve.wait_ge(x_factor_steps, i + 1)
                    dve.tensor_tensor(x_var[:, i], x_var[:, i], square_sum[:, i], ALU.add)\
                        .then_inc(x_factor_steps, 1)
                for i in range(LB):
                    dve.wait_ge(x_factor_steps, LB + i + 1)
                    dve.tensor_scalar(x_var[:, i], x_var[:, i], 0.0, 1.0 / D, ALU.max, ALU.mult)\
                        .then_inc(x_factor_steps, 1)
                for i in range(LB):
                    dve.wait_ge(x_std_ready, i + 1)
                    dve.reciprocal(x_var[:, i], x_var[:, i]).then_inc(x_factor_steps, 1)
                by_block = const["rstd"][:, 1].rearrange("p (i k) -> p k i", k=LB)
                for i in range(LB):
                    dve.wait_ge(x_factor_transposed, i + 1)
                    dve.tensor_copy(by_block[:, :, i * P:(i + 1) * P],
                                    ps_at[i][:, 0:L].rearrange("p (k i) -> p k i", k=LB))\
                        .then_inc(x_factor_steps, 1)
                dve.wait_ge(x_factor_steps, 5 * LB)

            dve.memset(eps[:], EPS).then_inc(sums_cleared, 1)
            dve.wait_ge(sums_cleared, 3)
            split(0, 0)
            run(dve, body)
            x_factors()

        @block.scalar
        def _(act):
            def high(it, d):
                n = it * ring + d
                wait(act, x_multiplied, (n - 1) * LB)
                for j in range(LB):
                    act.wait_ge(a_transposed, n * LB + j + 1)
                    act.activation(at_high[d % 2][:, j], ps_at[j][:, 0:L], ACT.Identity)\
                        .then_inc(a_high_done, 1)

            def copy(it, d):
                n = it * ring + d
                wait(act, x_stored[d % 2], (it * (ring // 2) + d // 2) * 16)
                wait(act, squares_summed, n - 1)
                for i in range(LB):
                    act.wait_ge(x_multiplied, n * LB + i + 1)
                    act.activation(x_out[d % 2][:, i], ps_x[i][:, 0:L], ACT.Identity)\
                        .then_inc(x_copied, 1)
                    act.activation(x_square[d % 2][:, i], ps_x[i][:, 0:L], ACT.Square)\
                        .then_inc(x_squared, 1)

            def body(it, last):
                for d in range(ring):
                    if exists(d + 1, last):
                        high(it, d + 1)
                    copy(it, d)

            high(0, 0)
            run(act, body)
            act.wait_ge(sums_cleared, 3)
            for i in range(LB):
                act.wait_ge(x_factor_steps, 2 * LB + i + 1)
                act.activation(x_var[:, i], x_var[:, i], ACT.Sqrt, bias=eps[:, 0:1]).then_inc(x_std_ready, 1)

        @block.gpsimd
        def _(pool):
            def add(it, d):
                n = it * ring + d
                pool.wait_ge(x_squared, (n + 1) * LB)
                wait(pool, squares_summed, n)
                pool.tensor_tensor(square_sum[:], square_sum[:], x_square[d % 2][:], ALU.add)\
                    .then_inc(squares_summed, 1)

            def body(it, last):
                for d in range(ring):
                    add(it, d)

            pool.memset(x_sum[:], 0.0).then_inc(sums_cleared, 1)
            pool.memset(square_sum[:], 0.0).then_inc(sums_cleared, 1)
            pool.wait_ge(sums_cleared, 3)
            run(pool, body)

        @block.tensor
        def _(pe):
            def transpose(it, d):
                n = it * ring + d
                pe.wait_ge(a_loaded[d % ring], (it + d // ring + 1) * 16)
                for j in range(LB):
                    wait(pe, a_low_done, (n - 1) * LB + j + 1)
                    for i in range(LB):
                        last = pe.transpose(ps_at[j][:, i * P:(i + 1) * P],
                                            a_raw[d % ring][:, i, j * P:(j + 1) * P], const["identity"][:])
                    last.then_inc(a_transposed, 1)

            def multiply(it, d):
                n = it * ring + d
                pe.wait_ge(a_low_done, (n + 1) * LB)
                pe.wait_ge(b_low_done, n + 1)
                for i in range(LB):
                    wait(pe, x_summed, (n - 1) * LB + i + 1)
                    cols = slice(i * P, (i + 1) * P)
                    terms = [(at_low, b_high, j) for j in range(LB)]
                    terms += [(at_high, part, j) for j in range(LB) for part in (b_low, b_high)]
                    for k, (left, right, j) in enumerate(terms):
                        last = pe.matmul(ps_x[i][:, 0:L], left[d % 2][:, j, cols], right[d % 2][:, j],
                                         start=k == 0, stop=k == len(terms) - 1)
                    last.then_inc(x_multiplied, 1)

            def body(it, last):
                for d in range(ring):
                    if exists(d + 1, last):
                        transpose(it, d + 1)
                    multiply(it, d)

            def transpose_factors():
                for i in range(LB):
                    pe.wait_ge(x_factor_steps, 3 * LB + i + 1)
                    for k in range(LB):
                        last = pe.transpose(ps_at[i][:, k * P:(k + 1) * P],
                                            x_var[:, i, k * P:(k + 1) * P], const["identity"][:])
                    last.then_inc(x_factor_transposed, 1)

            transpose(0, 0)
            run(pe, body)
            transpose_factors()


def finish(nc, z_flat, x_dram, out_flat, const):
    z_view = z_flat.rearrange("(n t p) c -> n p t c", p=P, t=CT)
    out_view = out_flat.rearrange("(n t p) c -> n p t c", p=P, t=CT)
    refine_steps = 2 + 3 * NEWTON_STEPS + 1
    factor_ops = MOMENT_STEPS + refine_steps

    with ExitStack() as ctx:
        def sb(name, shape, dt=F32):
            return ctx.enter_context(nc.sbuf_tensor(name, shape, dt))

        def sbs(name, shape, n):
            return [sb(f"{name}{k}", shape) for k in range(n)]

        def ps(name):
            return ctx.enter_context(nc.psum_tensor(name, [P, 512], F32))

        def sem(name):
            return ctx.enter_context(nc.semaphore(name))

        z = sbs("fz", [P, CT, D], CRING)
        xt = sbs("fxt", [D, CR * L], CRING)
        s_sum = sbs("s_sum", [P, CT, D], CRING)
        result = sbs("result", [P, CT, D], CRING)
        rstd_zx = sbs("rstd_zx_chunk", [P, 2, CT], CRING)
        stats = sbs("fstats", [P, FT, 6], FRING)
        work = [[sb(f"fwork{k}_{n}", [P, FT]) for n in range(3)] for k in range(FRING)]
        rstd = sbs("frstd", [P, FT], FRING)
        shift = sbs("fshift", [P, FT], FRING)
        zt = sbs("fzt", [D, L], 2)
        gate_arg = sbs("gate_arg", [P, L], 2)
        gate0 = sbs("gate0_", [P, L], 2)
        proj = sbs("proj", [P, L], 2)
        y_part = sbs("y_part", [P, L], 2)
        y = sbs("y", [P, L], 4)
        y_biased = sbs("y_biased", [P, L], 6)
        yt = sbs("yt", [D, L], 2)
        row_sum = sbs("row_sum", [D, 2], 2)
        right = sbs("right", [D, 2], 2)
        gate1 = sbs("gate1_", [D, L], 2)
        mixed = sbs("mixed", [D, L], 2)
        w_out = sbs("w_out", [D, D], 2)
        scaled = sbs("lnscaled", [P, L], 2)
        ps_z, ps_p, ps_q, ps_y, ps_g, ps_l, ps_o, normal = (
            ps(f"ps_{n}") for n in ("z", "p", "q", "y", "g", "l", "o", "normal"))

        z_loaded = [sem(f"fz_loaded{k}") for k in range(CRING)]
        x_loaded = [sem(f"fx_loaded{k}") for k in range(CRING)]
        stored = [sem(f"out_stored{k}") for k in range(CRING)]
        z_transposed = sem("z_transposed")
        z_copied = sem("z_copied")
        p_ready = sem("p_ready")
        q_ready = sem("q_ready")
        arg_ready = sem("arg_ready")
        gate0_ready = sem("gate0_ready")
        proj_ready = sem("proj_ready")
        y_part_ready = sem("y_part_ready")
        y_ready = sem("y_ready")
        y_biased_ready = sem("y_biased_ready")
        y_transposed = sem("y_transposed")
        y_copied = sem("y_copied")
        gate1_in_ready = sem("gate1_in_ready")
        left_ready = sem("left_ready")
        gate1_ready = sem("gate1_ready")
        right_ready = sem("right_ready")
        w_out_ready = sem("w_out_ready")
        mixed_ready = sem("mixed_ready")
        out_ready = sem("out_ready")
        summed = sem("summed")
        normal_ready = sem("normal_ready")
        scaled_ready = sem("scaled_ready")
        result_ready = sem("result_ready")
        s_measured = sem("s_measured")
        factor_steps = sem("ffactor_steps")
        chunk_factors = sem("chunk_factors")
        block = ctx.enter_context(nc.Block())
        bodies = L // BODY_R

        def run(engine, step):
            for b in range(2):
                for r in range(BODY_R):
                    step(b, r)
            with engine.Fori(2, bodies - 1) as it:
                for r in range(BODY_R):
                    step(it, r)
            for r in range(BODY_R + TO_RESULT):
                step(bodies - 1, r)

        def exists(it, r):
            return not isinstance(it, int) or 0 <= it * BODY_R + r < L

        def chunk_slot(r):
            return (r // CR) % CRING

        def dma_count(it, r):
            return (it + (r // CR) // CRING + 1) * 16

        @block.sync
        def _(sp):
            def load(it, c):
                rows = it * BODY_R + (c - CRING + 1) * CR
                wait(sp, y_ready, rows)
                sp.dma_start(z[c % CRING][:], z_view[it * CRING + c]).then_inc(z_loaded[c % CRING], 16)
                wait(sp, q_ready, rows)
                sp.dma_start(xt[c % CRING][:], x_dram[:, bass.ds((it * CRING + c) * CR * L, CR * L)])\
                    .then_inc(x_loaded[c % CRING], 16)

            def store(it, c):
                sp.wait_ge(result_ready, it * BODY_R + (c + 1) * CR)
                sp.dma_start(out_view[it * CRING + c], result[c % CRING][:])\
                    .then_inc(stored[c % CRING], 16)

            def body(it, first, last):
                for c in range(CRING):
                    if not last:
                        load(it, c + CRING)
                    if not (first and c < 2):
                        store(it, c - 2)

            for c in range(CRING):
                load(0, c)
            body(0, True, False)
            with sp.Fori(1, bodies - 1) as it:
                body(it, False, False)
            body(bodies - 1, False, True)
            store(bodies - 1, CRING - 2)
            store(bodies - 1, CRING - 1)
            for k in range(CRING):
                sp.wait_ge(stored[k], 16 * bodies)

        @block.tensor
        def _(pe):
            ident = const["identity"]

            def transpose_y(it, r):
                n = it * BODY_R + r
                pe.wait_ge(y_ready, n + 1)
                wait(pe, y_copied, n)
                for t in range(LB):
                    last = pe.transpose(ps_y[:, t * P:(t + 1) * P], y[r % 4][:, t * D:(t + 1) * D], ident[:])
                last.then_inc(y_transposed, 1)

            def transpose_z(it, r):
                n = it * BODY_R + r
                if r % CR == 0:
                    pe.wait_ge(z_loaded[chunk_slot(r)], dma_count(it, r))
                wait(pe, z_copied, n)
                for t in range(LB):
                    last = pe.transpose(ps_z[:, t * P:(t + 1) * P],
                                        z[chunk_slot(r)][:, (r % CR) * LB + t], ident[:])
                last.then_inc(z_transposed, 1)

            def project_z(it, r):
                n = it * BODY_R + r
                pe.wait_ge(z_copied, n + 1)
                wait(pe, arg_ready, n)
                for t in range(LB):
                    last = pe.matmul(ps_p[:, t * D:(t + 1) * D], zt[r % 2][:, t * P:(t + 1) * P],
                                     const["Wgo"][:], start=True, stop=True)
                last.then_inc(p_ready, 1)

            def project_x(it, r):
                n = it * BODY_R + r
                if r % CR == 0:
                    pe.wait_ge(x_loaded[chunk_slot(r)], dma_count(it, r))
                wait(pe, proj_ready, n)
                for t in range(LB):
                    at = (r % CR) * L + t * P
                    last = pe.matmul(ps_q[:, t * D:(t + 1) * D], xt[chunk_slot(r)][:, at:at + P],
                                     const["Wo"][:], start=True, stop=True)
                last.then_inc(q_ready, 1)

            def multiply_y(it, r):
                n = it * BODY_R + r
                pe.wait_ge(y_copied, n + 1)
                wait(pe, gate1_ready, n)
                wait(pe, right_ready, it * (BODY_R // 2) + r // 2)
                if r % 2 == 1:
                    pe.matmul(ps_g[:, L:L + 2], const["Wr"][:], row_sum[(r // 2) % 2][:], start=True, stop=True)
                pe.matmul(ps_g[:, 0:L], const["Wg"][:], yt[r % 2][:], start=True, stop=True)\
                    .then_inc(gate1_in_ready, 1)
                wait(pe, mixed_ready, n)
                pe.matmul(ps_l[:, 0:L], const["Wle"][:], yt[r % 2][:], start=True, stop=True)\
                    .then_inc(left_ready, 1)

            def multiply_out(it, r):
                n = it * BODY_R + r
                pe.wait_ge(mixed_ready, n + 1)
                pe.wait_ge(w_out_ready, n + 1)
                wait(pe, summed, n)
                for t in range(LB):
                    last = pe.matmul(ps_o[:, t * D:(t + 1) * D], mixed[r % 2][:, t * P:(t + 1) * P],
                                     w_out[r % 2][:], start=True, stop=True)
                last.then_inc(out_ready, 1)

            def step(it, r):
                for part, row in ((transpose_y, r - 1), (transpose_z, r + 2), (project_z, r + 1),
                                  (project_x, r + 1), (multiply_y, r - 1), (multiply_out, r - 3)):
                    if exists(it, row):
                        part(it, row)

            transpose_z(0, 0)
            transpose_z(0, 1)
            project_z(0, 0)
            project_x(0, 0)
            run(pe, step)

        @block.scalar
        def _(act):
            def copy_y(it, r):
                n = it * BODY_R + r
                act.wait_ge(y_transposed, n + 1)
                wait(act, left_ready, n - 1)
                act.activation(yt[r % 2][:], ps_y[:, 0:L], ACT.Identity, 
                               accum_out=row_sum[(r // 2) % 2][:, r % 2:r % 2 + 1])\
                    .then_inc(y_copied, 1)

            def copy_z(it, r):
                n = it * BODY_R + r
                act.wait_ge(z_transposed, n + 1)
                wait(act, p_ready, n - 1)
                act.activation(zt[r % 2][:], ps_z[:, 0:L], ACT.Identity).then_inc(z_copied, 1)

            def sigmoid0(it, r):
                n = it * BODY_R + r
                act.wait_ge(arg_ready, n + 1)
                wait(act, y_part_ready, n - 1)
                act.activation(gate0[r % 2][:], gate_arg[r % 2][:], ACT.Sigmoid).then_inc(gate0_ready, 1)

            def sigmoid1(it, r):
                n = it * BODY_R + r
                act.wait_ge(gate1_in_ready, n + 1)
                wait(act, mixed_ready, n - 1)
                act.activation(gate1[r % 2][:], ps_g[:, 0:L], ACT.Sigmoid, bias=const["bg"][:, 0:1])\
                    .then_inc(gate1_ready, 1)

            def right_sums(it, r):
                n = it * (BODY_R // 2) + r // 2
                act.wait_ge(gate1_in_ready, it * BODY_R + r + 2)
                wait(act, w_out_ready, 2 * (n - 1))
                act.activation(right[(r // 2) % 2][:], ps_g[:, L:L + 2], ACT.Identity, bias=const["br"][:, 0:1])\
                    .then_inc(right_ready, 1)

            def scale_w_out(it, r):
                n = it * BODY_R + r
                act.wait_ge(right_ready, it * (BODY_R // 2) + r // 2 + 1)
                wait(act, out_ready, n - 1)
                act.activation(w_out[r % 2][:], const["Wout"][:], ACT.Identity,
                               scale=right[(r // 2) % 2][:, r % 2:r % 2 + 1]).then_inc(w_out_ready, 1)

            def normalise(it, r):
                n = it * BODY_R + r
                k = chunk_slot(r)
                if r % FR == 0:
                    act.wait_ge(factor_steps, (it * FRING + r // FR + 1) * factor_ops)
                wait(act, scaled_ready, n)
                for t in range(LB):
                    m = (r % CR) * LB + t
                    f, at = (r // FR) % FRING, (r % FR) * LB + t
                    last = act.activation(normal[:, t * D:(t + 1) * D], s_sum[k][:, m], ACT.Identity,
                                          bias=shift[f][:, at:at + 1], scale=rstd[f][:, at:at + 1])
                last.then_inc(normal_ready, 1)

            def step(it, r):
                for part, row in ((copy_y, r - 1), (copy_z, r + 2), (right_sums, r - 3),
                                  (scale_w_out, r - 3), (normalise, r - TO_NORM), (sigmoid0, r + 1),
                                  (sigmoid1, r - 1)):
                    if exists(it, row) and (part is not right_sums or row % 2 == 0):
                        part(it, row)

            copy_z(0, 0)
            copy_z(0, 1)
            sigmoid0(0, 0)
            run(act, step)

        @block.vector
        def _(dve):
            def fetch_factors(it, c):
                dve.tensor_copy(rstd_zx[c % CRING][:], const["rstd"][:, :, bass.ds((it * CRING + c) * CT, CT)])\
                    .then_inc(chunk_factors, 1)

            def sum_moments(it, f):
                dve.wait_ge(s_measured, it * BODY_R + (f + 1) * FR)
                wait(dve, normal_ready, it * BODY_R + (f + 1 - FRING) * FR)
                k = f % FRING
                moments(dve, stats[k][:], [x[:] for x in work[k]], factor_steps,
                        (it * FRING + f) * factor_ops)

            def refine(it, f, n):
                k = f % FRING
                double_mean, variance, term = work[k]
                root = rstd[k]
                dve.wait_ge(factor_steps, (it * FRING + f) * factor_ops + MOMENT_STEPS + n)
                if n == 0:
                    done = dve.tensor_scalar(variance[:], variance[:], 1.0 / D, EPS, ALU.mult, ALU.add)
                elif n == 1:
                    done = dve.tensor_scalar(root[:].bitcast(I32), variance[:].bitcast(I32), -0.5, RSQRT_BITS,
                                             ALU.mult, ALU.add)
                elif n == refine_steps - 1:
                    done = dve.scalar_tensor_tensor(shift[k][:], double_mean[:], -0.5, root[:],
                                                    ALU.mult, ALU.mult)
                elif (n - 2) % 3 == 0:
                    done = dve.tensor_tensor(term[:], root[:], root[:], ALU.mult)
                elif (n - 2) % 3 == 1:
                    done = dve.scalar_tensor_tensor(term[:], term[:], -0.5, variance[:], ALU.mult, ALU.mult)
                else:
                    done = dve.scalar_tensor_tensor(root[:], term[:], 1.5, root[:], ALU.add, ALU.mult)
                done.then_inc(factor_steps, 1)

            def add_bias(it, r, bank, factor, bias, to, done):
                for t in range(LB):
                    m = (r % CR) * LB + t
                    last = dve.scalar_tensor_tensor(
                        to[r % 2][:, t * D:(t + 1) * D], bank[:, t * D:(t + 1) * D],
                        factor[:, m:m + 1], bias[:], ALU.mult, ALU.add)
                last.then_inc(done, 1)

            def gate_argument(it, r):
                n = it * BODY_R + r
                if r % CR == 0:
                    dve.wait_ge(chunk_factors, it * CRING + r // CR + 1)
                dve.wait_ge(p_ready, n + 1)
                wait(dve, gate0_ready, n - 1)
                add_bias(it, r, ps_p, rstd_zx[chunk_slot(r)][:, 0], const["bgo"], gate_arg, arg_ready)

            def projection(it, r):
                n = it * BODY_R + r
                dve.wait_ge(q_ready, n + 1)
                wait(dve, y_part_ready, n - 1)
                add_bias(it, r, ps_q, rstd_zx[chunk_slot(r)][:, 1], const["bo"], proj, proj_ready)

            def mix(it, r):
                n = it * BODY_R + r
                dve.wait_ge(left_ready, n + 1)
                dve.wait_ge(gate1_ready, n + 1)
                wait(dve, out_ready, n - 1)
                dve.scalar_tensor_tensor(mixed[r % 2][:], ps_l[:, 0:L], const["ble"][:, 0:1],
                                         gate1[r % 2][:], ALU.add, ALU.mult).then_inc(mixed_ready, 1)

            def add_residual(it, r):
                n = it * BODY_R + r
                k = chunk_slot(r)
                dve.wait_ge(out_ready, n + 1)
                dve.wait_ge(y_biased_ready, n + 1)
                if r % CR == 0:
                    wait(dve, normal_ready, n - (CRING - 1) * CR)
                m = (r % CR) * LB
                dve.tensor_tensor(s_sum[k][:, m:m + LB].rearrange("p t c -> p (t c)"), ps_o[:, 0:L],
                                  y_biased[r % 6][:], ALU.add).then_inc(summed, 1)

            def measure_s(it, r):
                n = it * BODY_R + r
                k = chunk_slot(r)
                dve.wait_ge(summed, n + 1)
                for t in range(LB):
                    last = dve.bn_stats(stats[(r // FR) % FRING][:, (r % FR) * LB + t],
                                        s_sum[k][:, (r % CR) * LB + t])
                last.then_inc(s_measured, 1)

            def scale_result(it, r):
                n = it * BODY_R + r
                dve.wait_ge(normal_ready, n + 1)
                wait(dve, result_ready, n - 1)
                dve.tensor_tensor(scaled[r % 2][:], normal[:, 0:L], const["ln_scale"][:],
                                  ALU.mult).then_inc(scaled_ready, 1)

            def step(it, r):
                parts = ((scale_result, r - TO_RESULT), (add_residual, r - TO_SUM), (mix, r - 2),
                         (measure_s, r - TO_SUM), (gate_argument, r + 1), (projection, r + 1))
                f = (r - TO_SUM - FR + 1) // FR
                since = (r - TO_SUM - FR + 1) % FR * len(parts)
                for p, (part, row) in enumerate(parts):
                    if exists(it, row):
                        part(it, row)
                    if exists(it, f * FR):
                        if since + p == 3:
                            sum_moments(it, f)
                        if 0 <= since + p - 4 < refine_steps:
                            refine(it, f, since + p - 4)
                if r % CR == 1 and exists(it, r + 3):
                    fetch_factors(it, (r + 3) // CR)

            fetch_factors(0, 0)
            gate_argument(0, 0)
            projection(0, 0)
            run(dve, step)

        @block.gpsimd
        def _(pool):
            def gate_projection(it, r):
                n = it * BODY_R + r
                pool.wait_ge(proj_ready, n + 1)
                pool.wait_ge(gate0_ready, n + 1)
                pool.tensor_tensor(y_part[r % 2][:], proj[r % 2][:], gate0[r % 2][:],
                                          ALU.mult).then_inc(y_part_ready, 1)

            def residual0(it, r):
                n = it * BODY_R + r
                wait(pool, y_transposed, n - 3)
                pool.wait_ge(y_part_ready, n + 1)
                m = (r % CR) * LB
                pool.tensor_tensor(y[r % 4][:], y_part[r % 2][:],
                                   z[chunk_slot(r)][:, m:m + LB].rearrange("p t c -> p (t c)"),
                                   ALU.add).then_inc(y_ready, 1)

            def add_out_bias(it, r):
                n = it * BODY_R + r
                pool.wait_ge(y_ready, n + 1)
                wait(pool, summed, n - 5)
                pool.tensor_tensor(y_biased[r % 6][:], y[r % 4][:], const["bout"][:],
                                          ALU.add).then_inc(y_biased_ready, 1)

            def shift_result(it, r):
                n = it * BODY_R + r
                k = chunk_slot(r)
                if r % CR == 0:
                    wait(pool, stored[k], dma_count(it, r) - 16)
                pool.wait_ge(scaled_ready, n + 1)
                m = (r % CR) * LB
                pool.tensor_tensor(result[k][:, m:m + LB].rearrange("p t c -> p (t c)"),
                                          scaled[r % 2][:], const["ln_bias"][:],
                                          ALU.add).then_inc(result_ready, 1)

            def step(it, r):
                for part, row in ((gate_projection, r + 1), (shift_result, r - TO_RESULT), (residual0, r + 1),
                                  (add_out_bias, r + 1)):
                    if exists(it, row):
                        part(it, row)

            gate_projection(0, 0)
            residual0(0, 0)
            add_out_bias(0, 0)
            run(pool, step)


_WEIGHTS = {"Wa": ("L0_conv_Wa", True), "Wga": ("L0_conv_Wga", True), "Wb": ("L0_conv_Wb", True),
            "Wgb": ("L0_conv_Wgb", True), "Wo": ("L0_conv_Wo", True), "Wgo": ("L0_conv_Wgo", True),
            "Wl": ("L1_conv_W_left", False), "We": ("L1_conv_W_eq", False),
            "Wr": ("L1_conv_W_right", False), "Wg": ("L1_conv_W_gate", False),
            "Wout": ("L1_conv_W_out", False)}
_VECTORS = {"norm_g": "L0_conv_norm_g", "norm_b": "L0_conv_norm_b", "normo_g": "L0_conv_normo_g",
            "normo_b": "L0_conv_normo_b", "ba": "L0_conv_ba", "bga": "L0_conv_bga", "bb": "L0_conv_bb",
            "bgb": "L0_conv_bgb", "bo": "L0_conv_bo", "bgo": "L0_conv_bgo", "bl": "L1_conv_b_left",
            "be": "L1_conv_b_eq", "br": "L1_conv_b_right", "bg": "L1_conv_b_gate",
            "bout": "L1_conv_b_out", "ln_scale": "L1_conv_ln_scale", "ln_bias": "L1_conv_ln_bias"}


def kernel(**inputs):
    import concourse.bacc as bacc
    import numpy as np
    from concourse.bass_utils import run_bass_kernel_spmd

    nc = bacc.Bacc("TRN2", target_bir_lowering=False, num_devices=1)
    arrays = {}

    def give(name, array):
        array = np.ascontiguousarray(array)
        arrays[name] = array
        return nc.dram_tensor(name, array.shape, mybir.dt.from_np(array.dtype), kind="ExternalInput").ap()

    x = give("x_in", np.asarray(inputs["x"]))
    w = {n: np.asarray(inputs[k]).T if turned else np.asarray(inputs[k])
         for n, (k, turned) in _WEIGHTS.items()}
    vec = {n: np.asarray(inputs[k]) for n, k in _VECTORS.items()}
    weights = give("weights", np.stack([w[n] for n in WEIGHTS], axis=1))
    columns = give("columns", np.stack([vec[n] for n in COLUMNS], axis=1))
    rows = give("rows", np.concatenate([vec[n] for n, copies in ROWS for _ in range(copies)])[None])
    out = nc.dram_tensor("out", (1, L, L, D), F32, kind="ExternalOutput").ap()
    bass_pair_layers(nc, x, weights, columns, rows, out)
    r = run_bass_kernel_spmd(nc, [arrays], core_ids=[0])
    return r.results[0]["out"]
```
